# Optimizing a Trainium2 kernel written in Bass

```python
import numpy as np
import jax
import jax.numpy as jnp

def _softmax(x, axis=-1):
    return jax.nn.softmax(x, axis=axis)

def _gelu(x):
    return jax.nn.gelu(x, approximate=True)

def _silu(x):
    return jax.nn.silu(x)

def _sigmoid(x):
    return jax.nn.sigmoid(x)

def _layernorm(x, axis=-1, eps=1e-05):
    m = jnp.mean(x, axis=axis, keepdims=True)
    v = jnp.var(x, axis=axis, keepdims=True)
    return (x - m) / jnp.sqrt(v + eps)

def _scatter_add(tgt, idx, src, axis=0):
    return tgt.at[idx].add(src)

def _segment_sum(src, seg, n):
    return jax.ops.segment_sum(src, seg, n)
kernel_name = 'mk_gnn_resnorm_d1_gnn_r32_58ccd0'

def setup_inputs(seed: int=0):
    np.random.seed(seed)
    _w = jnp.asarray

    def _rec_inputs():
        import jax
        import jax.numpy as jnp
        _gk = jax.random.key(seed)
        x = -0.0003713 + 1 * jax.random.normal(jax.random.fold_in(_gk, 1), (3125, 128), jnp.float32)
        _s = jax.random.randint(jax.random.fold_in(_gk, 2), (50000,), 0, 3125, jnp.int32)
        _d = jax.random.randint(jax.random.fold_in(_gk, 3), (50000,), 0, 3125, jnp.int32)
        _loop = jnp.arange(3125, dtype=jnp.int32)
        src = jnp.concatenate([_s, _d, _loop])
        dst = jnp.concatenate([_d, _s, _loop])
        _o = jnp.argsort(dst, stable=True)
        src = src[_o]
        dst = dst[_o]
        edge_attr_16 = 0.000268479 + 0.999861 * jax.random.normal(jax.random.fold_in(_gk, 11), (103125, 16), jnp.float32)
        edge_weight = jax.random.uniform(jax.random.fold_in(_gk, 13), (103125,), jnp.float32, 0.0, 9.99999)
        return (x, src, dst, edge_attr_16, edge_weight)
    x, src, dst, edge_attr_16, edge_weight = _rec_inputs()

    def _L0_gnn_setup():
        import jax, jax.numpy as jnp
        import numpy as np
        N_NODES = 3125
        N_EDGES = 20000
        HIDDEN = 128
        FILTERS = 128
        RADIAL = 50
        CUTOFF = 10.0

        def _linear_params(key, d_in, d_out):
            kw, kb = jax.random.split(key)
            bound = 1.0 / np.sqrt(d_in)
            W = jax.random.uniform(kw, (d_in, d_out), jnp.float32, -bound, bound)
            b = jax.random.uniform(kb, (d_out,), jnp.float32, -bound, bound)
            return (W, b)

        def _gaussian_smearing(d):
            offsets = jnp.linspace(0.0, CUTOFF, RADIAL, dtype=d.dtype)
            coeff = -0.5 / (offsets[1] - offsets[0]) ** 2
            diff = d[:, None] - offsets[None, :]
            return jnp.exp(coeff * diff * diff)
        key = jax.random.key(seed)
        ks = jax.random.split(key, 12)
        x = jax.random.normal(ks[0], (N_NODES, HIDDEN), jnp.float32)
        edge_index = jax.random.randint(ks[1], (2, N_EDGES), 0, N_NODES, jnp.int64 if jax.config.jax_enable_x64 else jnp.int32)
        edge_attr = jax.random.normal(ks[2], (N_EDGES, 16), jnp.float32)
        distances = jax.random.uniform(ks[3], (N_EDGES,), jnp.float32, 0.0, CUTOFF)
        Wm1, bm1 = _linear_params(ks[4], 2 * HIDDEN + RADIAL, FILTERS)
        Wm2, bm2 = _linear_params(ks[5], FILTERS, FILTERS)
        Wm3, bm3 = _linear_params(ks[6], FILTERS, HIDDEN)
        Wu1, bu1 = _linear_params(ks[7], 2 * HIDDEN, HIDDEN)
        Wu2, bu2 = _linear_params(ks[8], HIDDEN, HIDDEN)
        Wi1, bi1 = _linear_params(ks[9], HIDDEN, HIDDEN)
        Wi2, bi2 = _linear_params(ks[10], HIDDEN, HIDDEN)
        return {'x': x, 'edge_index': edge_index, 'edge_attr': edge_attr, 'distances': distances, 'Wm1': Wm1, 'bm1': bm1, 'Wm2': Wm2, 'bm2': bm2, 'Wm3': Wm3, 'bm3': bm3, 'Wu1': Wu1, 'bu1': bu1, 'Wu2': Wu2, 'bu2': bu2, 'Wi1': Wi1, 'bi1': bi1, 'Wi2': Wi2, 'bi2': bi2}
    _L0_gnn_all = _L0_gnn_setup()
    _L0_gnn_in = {k: v for k, v in _L0_gnn_all.items() if k in ('Wm1', 'bm1', 'Wm2', 'bm2', 'Wm3', 'bm3', 'Wu1', 'bu1', 'Wu2', 'bu2', 'Wi1', 'bi1', 'Wi2', 'bi2')}
    del _L0_gnn_all
    return {'x': x, 'src': src, 'dst': dst, 'edge_attr_16': edge_attr_16, 'edge_weight': edge_weight, 'L0_gnn_Wm1': _L0_gnn_in['Wm1'], 'L0_gnn_bm1': _L0_gnn_in['bm1'], 'L0_gnn_Wm2': _L0_gnn_in['Wm2'], 'L0_gnn_bm2': _L0_gnn_in['bm2'], 'L0_gnn_Wm3': _L0_gnn_in['Wm3'], 'L0_gnn_bm3': _L0_gnn_in['bm3'], 'L0_gnn_Wu1': _L0_gnn_in['Wu1'], 'L0_gnn_bu1': _L0_gnn_in['bu1'], 'L0_gnn_Wu2': _L0_gnn_in['Wu2'], 'L0_gnn_bu2': _L0_gnn_in['bu2'], 'L0_gnn_Wi1': _L0_gnn_in['Wi1'], 'L0_gnn_bi1': _L0_gnn_in['bi1'], 'L0_gnn_Wi2': _L0_gnn_in['Wi2'], 'L0_gnn_bi2': _L0_gnn_in['bi2']}

def reference(x, src, dst, edge_attr_16, edge_weight, L0_gnn_Wm1, L0_gnn_bm1, L0_gnn_Wm2, L0_gnn_bm2, L0_gnn_Wm3, L0_gnn_bm3, L0_gnn_Wu1, L0_gnn_bu1, L0_gnn_Wu2, L0_gnn_bu2, L0_gnn_Wi1, L0_gnn_bi1, L0_gnn_Wi2, L0_gnn_bi2):
    import jax
    import jax.numpy as jnp

    def _L0_gnn_ref(x, edge_index, edge_attr, distances, Wm1, bm1, Wm2, bm2, Wm3, bm3, Wu1, bu1, Wu2, bu2, Wi1, bi1, Wi2, bi2):
        import jax, jax.numpy as jnp
        import numpy as np
        N_NODES = 3125
        N_EDGES = 20000
        HIDDEN = 128
        FILTERS = 128
        RADIAL = 50
        CUTOFF = 10.0

        def _linear_params(key, d_in, d_out):
            kw, kb = jax.random.split(key)
            bound = 1.0 / np.sqrt(d_in)
            W = jax.random.uniform(kw, (d_in, d_out), jnp.float32, -bound, bound)
            b = jax.random.uniform(kb, (d_out,), jnp.float32, -bound, bound)
            return (W, b)

        def _gaussian_smearing(d):
            offsets = jnp.linspace(0.0, CUTOFF, RADIAL, dtype=d.dtype)
            coeff = -0.5 / (offsets[1] - offsets[0]) ** 2
            diff = d[:, None] - offsets[None, :]
            return jnp.exp(coeff * diff * diff)
        silu = jax.nn.silu
        radial = _gaussian_smearing(distances)
        row, col = (edge_index[0], edge_index[1])
        edge_features = jnp.concatenate([x[row], x[col], radial], axis=-1)
        h = silu(edge_features @ Wm1 + bm1)
        h = silu(h @ Wm2 + bm2)
        messages = h @ Wm3 + bm3
        out = jax.ops.segment_sum(messages, col, num_segments=x.shape[0])
        u = silu(jnp.concatenate([x, out], axis=-1) @ Wu1 + bu1)
        u = u @ Wu2 + bu2
        u = silu(u @ Wi1 + bi1)
        return u @ Wi2 + bi2
    edge_index = jnp.stack([src, dst])
    x = _layernorm(x + _L0_gnn_ref(x, edge_index, edge_attr_16, edge_weight, L0_gnn_Wm1, L0_gnn_bm1, L0_gnn_Wm2, L0_gnn_bm2, L0_gnn_Wm3, L0_gnn_bm3, L0_gnn_Wu1, L0_gnn_bu1, L0_gnn_Wu2, L0_gnn_bu2, L0_gnn_Wi1, L0_gnn_bi1, L0_gnn_Wi2, L0_gnn_bi2), axis=-1)
    return x

_drawn_inputs = setup_inputs


def setup_inputs(seed=0):
    import zlib

    import numpy as np

    out = dict(_drawn_inputs(seed))
    spreads = {}
    factors = {'edge_weight': 64.0,
     'L0_gnn_bm1': 8.0,
     'L0_gnn_bm2': 4.779,
     'L0_gnn_bu1': 28.237,
     'L0_gnn_bu2': 7.143,
     'L0_gnn_bi1': 4.484}
    for name, (base, spread) in spreads.items():
        noise = np.random.default_rng([zlib.crc32(name.encode()), seed]).standard_normal(out[name].shape)
        drawn = base * np.exp(spread * noise) if base else spread * noise
        out[name] = jnp.asarray(drawn.astype(out[name].dtype))
    for name, factor in factors.items():
        out[name] = (out[name] * factor).astype(out[name].dtype)
    return out
```

```python
from contextlib import ExitStack

import concourse.bass as bass
from concourse import mybir

F32 = mybir.dt.float32
BF16 = mybir.dt.bfloat16
I32 = mybir.dt.int32
ALU = mybir.AluOpType
ACT = mybir.ActivationFunctionType
AX = mybir.AxisListType

P = 128
RADIAL = 50
CUTOFF = 10.0
EPS = 1e-5
WIN = 64
TILE = 128
HALF = 512
HT = HALF // TILE
GROUP = 2 * HALF
GT = GROUP // TILE
FAR = 8191


def gnn_kernel(nc, x, src, dst, dist, Wm1, bm1, Wm2, bm2, Wm3, bm3, Wu1, bu1, Wu2, bu2, Wi1, bi1,
               Wi2, bi2, out, force_general=False):
    N, D = x.shape
    E = src.shape[0]
    assert D == P
    NB = -(-N // P)
    NPAD = NB * P
    NW = -(-N // WIN)
    NCOL = NW * WIN
    G = -(-E // GROUP)
    H = 2 * G
    FULL = E // GROUP
    REST = E - FULL * GROUP
    assert G == FULL + 1 and G % 2 == 1 and G >= 5 and G <= P
    LOOPS = (H - 6) // 4
    LASTN = N - (NB - 1) * P
    NCH = -(-NCOL // HALF)
    chunk = [(HALF * c, min(HALF, NCOL - HALF * c)) for c in range(NCH)]
    chunk_blocks = [range(4 * c, min(4 * c + 4, NB)) for c in range(NCH)]

    with ExitStack() as ctx:
        def sb(name, shape, dt=F32):
            return ctx.enter_context(nc.sbuf_tensor(name, shape, dt))

        def sem(name):
            return ctx.enter_context(nc.semaphore(name))

        p_rows = nc.dram_tensor("p_rows", (NPAD, D), F32).ap()
        q_rows = nc.dram_tensor("q_rows", (NPAD, D), F32).ap()
        rel_rows = nc.dram_tensor("rel_rows", (G, GROUP), F32).ap()
        base_row = nc.dram_tensor("base_row", (1, G), I32).ap()

        bank = [ctx.enter_context(nc.psum_tensor(f"bank{n}", [P, HALF], F32)) for n in range(8)]
        pre_ps, l2_ps, agg_ps = bank[0:2], bank[2:4], bank[4:6]

        w1a = sb("w1a", [P, D])
        w1b = sb("w1b", [P, D])
        w2 = sb("w2", [P, D])
        w2half = sb("w2half", [P, D])
        w3 = sb("w3", [P, D])
        w3t = sb("w3t", [P, D])
        wu1a = sb("wu1a", [P, D])
        wu1b = sb("wu1b", [P, D])
        wu2 = sb("wu2", [P, D])
        wu2t = sb("wu2t", [P, D])
        wi1 = sb("wi1", [P, D])
        wi2 = sb("wi2", [P, D])
        w3u = sb("w3u", [P, D])
        wui = sb("wui", [P, D])
        b1_all = sb("b1_all", [P, D])
        bi2_all = sb("bi2_all", [P, D])
        cols = sb("cols", [P, 4])
        b3u = sb("b3u", [P, 1])
        bui = sb("bui", [P, 1])
        b2_row = sb("b2_row", [1, D])
        b2_part = sb("b2_part", [1, 3, D], BF16)
        b2_left = sb("b2_left", [1, 2, D])
        b2_rhs = sb("b2_rhs", [3, HT, D], BF16)
        ones_bf = sb("ones_bf", [P, P], BF16)
        ones_f = sb("ones_f", [P, P])
        ident = sb("ident", [P, P])
        lane = sb("lane", [P, 1])
        lane_i = sb("lane_i", [P, 1], I32)
        offset = sb("offset", [P, 1])
        win_i = sb("win_i", [P, WIN], I32)
        win = sb("win", [P, WIN])
        eps = sb("eps", [P, 1])

        xn = sb("xn", [P, NB, D])
        xt = sb("xt", [P, NPAD])
        y = xt[:, :].rearrange("p (b d) -> p b d", d=D)
        p_out = sb("p_out", [P, NB, D])
        q_out = sb("q_out", [P, NB, D])
        s1 = p_out[:, :, :].rearrange("p b d -> p (b d)")
        s2 = q_out[:, :, :].rearrange("p b d -> p (b d)")
        xu = sb("xu", [P, NPAD])
        agg = sb("agg", [P, 2, NCOL])

        src_i = sb("src_i", [P, GROUP], I32)
        dst_i = sb("dst_i", [P, GROUP], I32)
        src_f = sb("src_f", [P, GROUP])
        dst_f = sb("dst_f", [P, GROUP])
        least = sb("least", [P, 2])
        most = sb("most", [P, 2])
        base = sb("base", [P, 3])
        base_i = sb("base_i", [P, 1], I32)
        wide = sb("wide", [P, 2])
        sorted_i = sb("sorted_i", [P, 1], I32)
        base_sb = sb("base_sb", [1, G], I32)
        src_col = sb("src_col", [P, G + 1, GT], I32)
        rel_col = sb("rel_col", [P, G + 1, GT])

        index = sb("index", [P, 4, HT], I32)
        rows = sb("rows", [P, 4, HT, D])
        dist_b = sb("dist_b", [WIN, 2, GROUP])
        rel_b = sb("rel_b", [P, 2, GROUP])
        feat = sb("feat", [P, 2, GROUP])
        left = sb("left", [P, 2, D])
        hot = sb("hot", [P, 2, GT, WIN])
        th1 = sb("th1", [P, 2, HALF])
        h1 = sb("h1", [P, 2, HALF])
        th2 = sb("th2", [P, 2, HALF])
        h2 = sb("h2", [P, 2, HALF])
        stats = sb("stats", [P, NB, 6])
        mv = sb("mv", [P, NB, 2])
        std = sb("std", [P, NB])
        rstd = sb("rstd", [P, NB])
        res = p_out

        x_loaded = [sem(f"x_loaded{n}") for n in range(2)]
        first_weights = sem("first_weights")
        weights_loaded = sem("weights_loaded")
        edges_loaded = sem("edges_loaded")
        dst_loaded = sem("dst_loaded")
        b2_loaded = sem("b2_loaded")
        b2_placed = sem("b2_placed")
        pool_const = sem("pool_const")
        pads_set = sem("pads_set")
        zeros_set = sem("zeros_set")
        v_chain = sem("v_chain")
        xt_ps_done = sem("xt_ps_done")
        xt_done = sem("xt_done")
        pq_ps_done = sem("pq_ps_done")
        pq_done = sem("pq_done")
        p_stored = sem("p_stored")
        q_stored = sem("q_stored")
        tables_ps = sem("tables_ps")
        tables_done = sem("tables_done")
        wide_done = sem("wide_done")
        wide_ps = sem("wide_ps")
        base_done = sem("base_done")
        rel_done = sem("rel_done")
        rel_stored = sem("rel_stored")
        base_stored = sem("base_stored")
        base_loaded = sem("base_loaded")
        turn_ps = sem("turn_ps")
        turned = sem("turned")
        fold_ps = sem("fold_ps")
        folded = sem("folded")
        xu_ps = sem("xu_ps")
        xu_done = sem("xu_done")
        lane_done = sem("lane_done")
        index_ready = sem("index_ready")
        index_seen = sem("index_seen")
        gathered = [sem(f"gathered{n}") for n in range(4)]
        dist_loaded = [sem(f"dist_loaded{n}") for n in range(2)]
        rel_loaded = [sem(f"rel_loaded{n}") for n in range(2)]
        q_loaded = [sem(f"q_loaded{n}") for n in range(2)]
        square_done = sem("square_done")
        radial_ready = sem("radial_ready")
        one_hot_ready = sem("one_hot_ready")
        pre_done = sem("pre_done")
        tanh1_done = sem("tanh1_done")
        h1_ready = sem("h1_ready")
        l2_done = sem("l2_done")
        tanh2_done = sem("tanh2_done")
        h2_ready = sem("h2_ready")
        hot_ready = sem("hot_ready")
        seg_done = sem("seg_done")
        agg_added = sem("agg_added")
        gen_added = sem("gen_added")
        gen_index_ready = sem("gen_index_ready")
        gen_gathered = sem("gen_gathered")
        gen_dist_loaded = sem("gen_dist_loaded")
        gen_square_done = sem("gen_square_done")
        gen_radial_ready = sem("gen_radial_ready")
        gen_rel_loaded = sem("gen_rel_loaded")
        gen_rel_ready = sem("gen_rel_ready")
        gen_q_loaded = sem("gen_q_loaded")
        gen_hot_ready = sem("gen_hot_ready")
        gen_pre_done = sem("gen_pre_done")
        gen_tanh1_done = sem("gen_tanh1_done")
        gen_h1_ready = sem("gen_h1_ready")
        gen_l2_done = sem("gen_l2_done")
        gen_tanh2_done = sem("gen_tanh2_done")
        gen_h2_ready = sem("gen_h2_ready")
        gen_seg_done = sem("gen_seg_done")
        edges_done = sem("edges_done")
        deg_done = sem("deg_done")
        a_ps = sem("a_ps")
        z1_done = sem("z1_done")
        s1_done = sem("s1_done")
        b_ps = sem("b_ps")
        s2_done = sem("s2_done")
        c_ps = sem("c_ps")
        y_done = sem("y_done")
        stats_done = sem("stats_done")
        mv_done = sem("mv_done")
        std_done = sem("std_done")
        rstd_done = sem("rstd_done")
        res_done = sem("res_done")
        out_stored = sem("out_stored")
        xb_done = sem("xb_done")

        block = ctx.enter_context(nc.Block())
        XA = 12
        dst_whole = dst[0:FULL * GROUP].rearrange("(g e) -> g e", e=GROUP)
        src_whole = src[0:FULL * GROUP].rearrange("(g e) -> g e", e=GROUP)
        dst_rest = dst[FULL * GROUP:E].rearrange("(a e) -> a e", a=1)
        src_rest = src[FULL * GROUP:E].rearrange("(a e) -> a e", a=1)
        dist_row = dist.rearrange("(a e) -> a e", a=1)

        def row_of(v):
            return v.rearrange("(a d) -> a d", a=1)

        def col_of(v):
            return v.rearrange("(d a) -> d a", a=1)

        def is_fast(eng):
            return eng.value_load(sorted_i[0:1, 0:1], min_val=0, max_val=1)

        @block.sync
        def _(sp):
            sp.dma_start(xn[:, 0:XA, :], x[0:XA * P, :].rearrange("(b p) d -> p b d", p=P)).then_inc(x_loaded[0], 16)
            sp.wait_ge(zeros_set, 2)
            sp.dma_start(xn[:, XA:NB - 1, :],
                         x[XA * P:(NB - 1) * P, :].rearrange("(b p) d -> p b d", p=P)).then_inc(x_loaded[1], 16)
            sp.dma_start(xn[0:LASTN, NB - 1, :], x[(NB - 1) * P:N, :]).then_inc(x_loaded[1], 16)
            sp.dma_start(left[0:RADIAL, 0, :], Wm1[2 * D:2 * D + RADIAL, :]).then_inc(weights_loaded, 16)
            sp.dma_start(left[0:RADIAL, 1, :], Wm1[2 * D:2 * D + RADIAL, :]).then_inc(weights_loaded, 16)
            for tile_, dram in ((w2, Wm2), (w3, Wm3), (wu1a, Wu1[0:D, :]), (wu1b, Wu1[D:2 * D, :]),
                                (wu2, Wu2), (wi1, Wi1), (wi2, Wi2),
                                (bi2_all, row_of(bi2).broadcast_to([P, D]))):
                sp.dma_start(tile_[:, :], dram).then_inc(weights_loaded, 16)
            for n, v in enumerate((bm3, bu2, bu1, bi1)):
                sp.dma_start(cols[:, n:n + 1], col_of(v)).then_inc(weights_loaded, 16)
            sp.wait_ge(b2_loaded, 17)
            for n in range(3):
                sp.dma_start(b2_rhs[n:n + 1, :, :],
                             b2_part[:, n:n + 1, :].broadcast_to([1, HT, D])).then_inc(b2_placed, 16)
            for c in range(NCH):
                bs = slice(chunk_blocks[c].start, chunk_blocks[c].stop)
                rows_of = slice(bs.start * P, bs.stop * P)
                sp.wait_ge(pq_done, bs.stop)
                sp.dma_start(p_rows[rows_of, :].rearrange("(b p) d -> p b d", p=P), p_out[:, bs, :]).then_inc(p_stored, 16)
                sp.dma_start(q_rows[rows_of, :].rearrange("(b p) d -> p b d", p=P), q_out[:, bs, :]).then_inc(q_stored, 16)
            sp.wait_ge(base_done, 1)
            sp.dma_start(base_row.rearrange("a g -> g a"), base_i[0:G, :]).then_inc(base_stored, 16)
            sp.wait_ge(rel_done, 1)
            sp.dma_start(rel_rows, dst_f[0:G, :]).then_inc(rel_stored, 16)
            sp.wait_ge(base_stored, 16)
            sp.dma_start(base_sb[:, :], base_row).then_inc(base_loaded, 16)
            sp.wait_ge(rel_stored, 16)
            sp.wait_ge(q_stored, 16 * NCH)
            sp.wait_ge(base_loaded, 16)
            sp.wait_ge(zeros_set, 3)

            def load_group(g, s, g_before, edges=GROUP):
                b = sp.value_load(base_sb[0:1, bass.ds(g, 1)], min_val=0, max_val=N - WIN)
                if g_before is not None:
                    sp.wait_ge(square_done, g_before)
                sp.dma_start(dist_b[:, s, 0:edges],
                             dist_row[:, bass.ds(g * GROUP, edges)].broadcast_to([WIN, edges])).then_inc(dist_loaded[s], 16)
                if g_before is not None:
                    sp.wait_ge(one_hot_ready, g_before)
                sp.dma_start(rel_b[WIN:P, s, :],
                             rel_rows[bass.ds(g, 1), :].broadcast_to([WIN, GROUP])).then_inc(rel_loaded[s], 16)
                if g_before is not None:
                    sp.wait_ge(pre_done, g_before)
                sp.dma_start(left[WIN:P, s, :], q_rows[bass.ds(b, WIN), :]).then_inc(q_loaded[s], 16)

            def general_loads(g, edges):
                sp.wait_ge(gen_added, g * NW + 1)
                sp.dma_start(dist_b[:, 0, 0:edges], dist_row[:, bass.ds(g * GROUP, edges)].broadcast_to([WIN, edges]))\
                    .then_inc(gen_dist_loaded, 16)
                sp.dma_start(rel_b[WIN:P, 0, :], rel_rows[bass.ds(g, 1), :].broadcast_to([WIN, GROUP]))\
                    .then_inc(gen_rel_loaded, 16)
                with sp.Fori(0, NW) as w:
                    sp.wait_ge(gen_added, w + (g * NW + 1))
                    sp.dma_start(left[WIN:P, 0, :], q_rows[bass.ds(w * WIN, WIN), :]).then_inc(gen_q_loaded, 16)

            with sp.If(is_fast(sp) > 0):
                load_group(0, 0, None)
                load_group(1, 1, None)
                with sp.Fori(0, (G - 3) // 2) as i:
                    load_group(i * 2 + 2, 0, i * 4 + 2)
                    load_group(i * 2 + 3, 1, i * 4 + 4)
                load_group(G - 1, (G - 1) % 2, 2 * (G - 1) - 2, REST)
            with sp.Else():
                with sp.Fori(0, FULL) as g:
                    general_loads(g, GROUP)
                general_loads(FULL, REST)

            for c in range(NCH):
                bs = chunk_blocks[c]
                sp.wait_ge(res_done, bs.stop)
                whole = min(bs.stop, NB - 1)
                if whole > bs.start:
                    sp.dma_start(out[bs.start * P:whole * P, :].rearrange("(b p) d -> p b d", p=P),
                                 res[:, bs.start:whole, :]).then_inc(out_stored, 16)
            sp.dma_start(out[(NB - 1) * P:N, :], res[0:LASTN, NB - 1, :]).then_inc(out_stored, 16)
            sp.wait_ge(out_stored, 16 * ((NB - 1 + 3) // 4 + 1))

        @block.gpsimd
        def _(pool):
            nc.gpsimd.memset(ident[:, :], 0.0).then_inc(pool_const, 1)
            pool.wait_ge(pool_const, 1)
            nc.gpsimd.affine_select(out=ident[:, :], in_=ident[:, :], compare_op=ALU.not_equal, fill=1.0,
                                    base=0, pattern=[[-1, P]], channel_multiplier=1).then_inc(pool_const, 1)
            nc.gpsimd.iota(lane_i[:, :], pattern=[[0, 1]], base=-WIN, channel_multiplier=1).then_inc(pool_const, 1)
            nc.gpsimd.iota(win_i[:, :], pattern=[[1, WIN]], base=0, channel_multiplier=0).then_inc(pool_const, 1)
            nc.gpsimd.memset(ones_bf[:, :], 1.0).then_inc(pool_const, 1)
            nc.gpsimd.memset(ones_f[:, :], 1.0).then_inc(pool_const, 1)
            pool.wait_ge(p_stored, 16 * NCH)
            pool.wait_ge(base_done, 1)

            def gather(h, s):
                pool.wait_ge(index_ready, h + 1)
                pool.sem_inc(index_seen, 1)
                for j in range(HT):
                    nc.gpsimd.indirect_dma_start(
                        rows[:, s, j, :], None, p_rows,
                        bass.IndirectOffsetOnAxis(ap=index[:, s, j:j + 1], axis=0)).then_inc(gathered[s], 16)

            with pool.If(is_fast(pool) > 0):
                with pool.Fori(0, H // 4) as i:
                    for k in range(4):
                        gather(i * 4 + k, k)
                for h in range(H // 4 * 4, H):
                    gather(h, h % 4)
            with pool.Else():
                with pool.Fori(0, G) as g:
                    pool.wait_ge(gen_index_ready, g + 1)
                    pool.sem_inc(index_seen, 1)
                    for s in range(2):
                        for j in range(HT):
                            nc.gpsimd.indirect_dma_start(
                                rows[:, s, j, :], None, p_rows,
                                bass.IndirectOffsetOnAxis(ap=index[:, s, j:j + 1], axis=0)).then_inc(gen_gathered, 16)

        @block.tensor
        def _(pe):
            pe.wait_ge(pool_const, 2)
            def turn_x(c):
                bs = chunk_blocks[c]
                if c >= 2:
                    pe.wait_ge(xt_done, c - 1)
                for b in bs:
                    if b == 0:
                        pe.wait_ge(x_loaded[0], 16)
                    if b == XA:
                        pe.wait_ge(x_loaded[1], 32)
                    mm = nc.tensor.transpose(bank[c % 2][:, (b - bs.start) * P:(b - bs.start + 1) * P],
                                             xn[:, b, :], ident[:, :])
                mm.then_inc(xt_ps_done, 1)

            def make_pq(c):
                pe.wait_ge(xt_done, c + 1)
                if c == 0:
                    pe.wait_ge(first_weights, 48)
                for b in chunk_blocks[c]:
                    if b >= 4:
                        pe.wait_ge(pq_done, b - 3)
                    for n, w in enumerate((w1a, w1b)):
                        mm = nc.tensor.matmul(bank[2 + b % 4][:, n * D:(n + 1) * D], xt[:, b * P:(b + 1) * P], w[:, :],
                                              start=True, stop=True)
                    mm.then_inc(pq_ps_done, 1)

            turn_x(0)
            for c in range(NCH):
                if c + 1 < NCH:
                    turn_x(c + 1)
                make_pq(c)
                if c == 1:
                    pe.wait_ge(pool_const, 6)
                    pe.wait_ge(wide_done, 1)
                    nc.tensor.matmul(bank[6][:, 0:1], ones_f[0:G, :], wide[0:G, 0:1], start=True, stop=True).then_inc(wide_ps, 1)
            pe.wait_ge(rel_done, 1)
            for n, table in enumerate((src_f, dst_f)):
                for j in range(GT):
                    mm = nc.tensor.transpose(bank[6 + j // 4][:, (j % 4) * G:(j % 4 + 1) * G],
                                             table[0:G, j * TILE:(j + 1) * TILE], ident[0:G, 0:G])
                mm.then_inc(tables_ps, 1)
                pe.wait_ge(tables_done, 2 * n + 2)
            pe.wait_ge(weights_loaded, 16 * 14)
            nc.tensor.transpose(bank[6][:, 0:D], w3[:, :], ident[:, :])
            nc.tensor.transpose(bank[6][:, D:2 * D], wu2[:, :], ident[:, :]).then_inc(turn_ps, 1)
            pe.wait_ge(turned, 2)
            nc.tensor.matmul(bank[7][:, 0:D], w3t[:, :], wu1b[:, :], start=True, stop=True)
            nc.tensor.matmul(bank[7][:, D:2 * D], wu2t[:, :], wi1[:, :], start=True, stop=True)
            nc.tensor.matmul(bank[7][:, 2 * D:2 * D + 1], wu1b[:, :], cols[:, 0:1], start=True, stop=True)
            nc.tensor.matmul(bank[7][:, 2 * D + 1:2 * D + 2], wi1[:, :], cols[:, 1:2], start=True, stop=True).then_inc(fold_ps, 1)

            def update_x(c):
                n0, n = chunk[c]
                if c >= 1:
                    pe.wait_ge(xu_done, c)
                nc.tensor.matmul(bank[6][:, 0:n], wu1a[:, :], xt[:, n0:n0 + n], start=True, stop=True).then_inc(xu_ps, 1)

            for c in range(NCH):
                update_x(c)

            pe.wait_ge(base_done, 1)
            pe.wait_ge(b2_placed, 48)

            def sum_tile(s, h2_tile, t):
                nc.tensor.matmul(agg_ps[s][:, 0:WIN], h2_tile, hot[:, s, t, :],
                                 start=t == 0, stop=t == GT - 1, skip_group_check=True)
                return nc.tensor.matmul(agg_ps[s][:, WIN:2 * WIN], ones_bf[:, :],
                                        hot[:, s, t, :].bitcast(BF16)[:, 1:2 * WIN:2],
                                        start=False, stop=t == GT - 1, skip_group_check=True)

            def first_layer(h, g2, k):
                s = (k // 2) % 2
                pe.wait_ge(radial_ready, h + 1)
                pe.wait_ge(one_hot_ready, h + 1)
                if k % 2 == 0:
                    pe.wait_ge(q_loaded[s], g2 * 16 + 16)
                if not isinstance(h, int) or h >= 2:
                    pe.wait_ge(h1_ready, h - 1)
                at = (k % 2) * HALF
                nc.tensor.matmul(pre_ps[k % 2][:, :], left[:, s, :], feat[:, s, at:at + HALF], start=True, stop=True)
                pe.wait_ge(gathered[k], g2 * (16 * HT) + 16 * HT)
                for j in range(HT):
                    mm = nc.tensor.matmul(pre_ps[k % 2][:, j * TILE:(j + 1) * TILE], rows[:, k, j, :], ident[:, :],
                                          start=False, stop=True, skip_group_check=True)
                mm.then_inc(pre_done, 1)

            def second_layer(h, k):
                pe.wait_ge(h1_ready, h + 1)
                if not isinstance(h, int) or h >= 2:
                    pe.wait_ge(h2_ready, h - 1)
                nc.tensor.matmul(l2_ps[k % 2][:, :], ones_bf[0:3, :], b2_rhs[:, :, :].rearrange("p t d -> p (t d)"),
                                 start=True, stop=True)
                for j in range(HT):
                    mm = nc.tensor.matmul(l2_ps[k % 2][:, j * D:(j + 1) * D], h1[:, k % 2, j * TILE:(j + 1) * TILE],
                                          w2half[:, :], start=False, stop=True, skip_group_check=True)
                mm.then_inc(l2_done, 1)

            def sum_over_dst(h, g, k):
                s = (k // 2) % 2
                pe.wait_ge(h2_ready, h + 1)
                if k % 2 == 0:
                    pe.wait_ge(hot_ready, g + 1)
                    if not isinstance(g, int) or g >= 2:
                        pe.wait_ge(agg_added, g - 1)
                for j in range(HT):
                    mm = sum_tile(s, h2[:, k % 2, j * D:(j + 1) * D], (k % 2) * HT + j)
                mm.then_inc(seg_done, 1)

            def step(h, g, g2, k):
                if not isinstance(h, int) or h < H:
                    first_layer(h, g2, k)
                if not isinstance(h, int) or 1 <= h <= H:
                    second_layer(h - 1, (k - 1) % 4)
                if not isinstance(h, int) or h >= 2:
                    sum_over_dst(h - 2, g - 1, (k - 2) % 4)

            def general_matmuls():
                with pe.Fori(0, G) as g:
                    with pe.Fori(0, NW) as w:
                        pe.wait_ge(gen_gathered, g * (16 * GT) + 16 * GT)
                        pe.wait_ge(gen_radial_ready, g + 1)
                        pe.wait_ge(gen_q_loaded, (g * NW + w + 1) * 16)
                        pe.wait_ge(gen_hot_ready, g * NW + w + 1)
                        for s in range(2):
                            nc.tensor.matmul(pre_ps[s][:, :], left[:, 0, :], feat[:, 0, s * HALF:(s + 1) * HALF],
                                             start=True, stop=True)
                            for j in range(HT):
                                mm = nc.tensor.matmul(pre_ps[s][:, j * TILE:(j + 1) * TILE], rows[:, s, j, :],
                                                      ident[:, :], start=False, stop=True, skip_group_check=True)
                        mm.then_inc(gen_pre_done, 1)
                        pe.wait_ge(gen_h1_ready, g * NW + w + 1)
                        for s in range(2):
                            nc.tensor.matmul(l2_ps[s][:, :], ones_bf[0:3, :],
                                             b2_rhs[:, :, :].rearrange("p t d -> p (t d)"), start=True, stop=True)
                            for j in range(HT):
                                mm = nc.tensor.matmul(l2_ps[s][:, j * D:(j + 1) * D],
                                                      h1[:, s, j * TILE:(j + 1) * TILE], w2half[:, :],
                                                      start=False, stop=True, skip_group_check=True)
                        mm.then_inc(gen_l2_done, 1)
                        pe.wait_ge(gen_h2_ready, g * NW + w + 1)
                        for t in range(GT):
                            mm = sum_tile(0, h2[:, t // HT, t % HT * D:(t % HT + 1) * D], t)
                        mm.then_inc(gen_seg_done, 1)

            with pe.If(is_fast(pe) > 0):
                for h in range(4):
                    step(h, h // 2, h // 4, h)
                with pe.Fori(0, LOOPS) as i:
                    for k in range(4):
                        step(i * 4 + (4 + k), i * 2 + (2 + k // 2), i + 1, k)
                for h in range(H - 2, H + 2):
                    step(h, h // 2, h // 4, h % 4)
            with pe.Else():
                general_matmuls()

            def update_a(c):
                n0, n = chunk[c]
                if c >= 2:
                    pe.wait_ge(z1_done, c - 1)
                nc.tensor.matmul(bank[c % 2][:, 0:n], w3u[:, :], agg[:, 0, n0:n0 + n], start=True, stop=True).then_inc(a_ps, 1)

            def update_b(c):
                n0, n = chunk[c]
                pe.wait_ge(s1_done, c + 1)
                nc.tensor.matmul(bank[2 + c % 2][:, 0:n], wui[:, :], s1[:, n0:n0 + n], start=True, stop=True).then_inc(b_ps, 1)

            def update_c(c):
                pe.wait_ge(s2_done, c + 1)
                if c >= 2:
                    pe.wait_ge(y_done, c - 1)
                for n, b in enumerate(chunk_blocks[c]):
                    m = min(P, NCOL - b * P)
                    mm = nc.tensor.matmul(bank[4 + c % 2][0:m, n * D:(n + 1) * D], s2[:, b * P:b * P + m], wi2[:, :],
                                          start=True, stop=True)
                mm.then_inc(c_ps, 1)

            pe.wait_ge(edges_done, 1)
            for c in range(NCH + 2):
                if c < NCH:
                    update_a(c)
                if 1 <= c <= NCH:
                    update_b(c - 1)
                if c >= 2:
                    update_c(c - 2)

        @block.scalar
        def _(act):
            act.wait_ge(pads_set, 2)
            act.dma_start(dst_i[0:FULL, :], dst_whole).then_inc(dst_loaded, 16)
            act.dma_start(dst_i[FULL:G, 0:REST], dst_rest).then_inc(dst_loaded, 16)
            act.dma_start(w1a[:, :], Wm1[0:D, :]).then_inc(first_weights, 16)
            act.dma_start(w1b[:, :], Wm1[D:2 * D, :]).then_inc(first_weights, 16)
            act.dma_start(b1_all[:, :], row_of(bm1).broadcast_to([P, D])).then_inc(first_weights, 16)
            act.dma_start(src_i[0:FULL, :], src_whole).then_inc(edges_loaded, 16)
            act.dma_start(src_i[FULL:G, 0:REST], src_rest).then_inc(edges_loaded, 16)
            act.dma_start(b2_row[:, :], row_of(bm2)).then_inc(b2_loaded, 16)
            for c in range(NCH):
                n = len(chunk_blocks[c]) * P
                act.wait_ge(xt_ps_done, c + 1)
                nc.scalar.activation(xt[:, c * HALF:c * HALF + n], bank[c % 2][:, 0:n], ACT.Copy).then_inc(xt_done, 1)
            for c in range(NCH):
                n0, n = chunk[c]
                if c == 0:
                    act.wait_ge(weights_loaded, 16 * 14)
                act.wait_ge(xu_ps, c + 1)
                nc.scalar.activation(xu[:, n0:n0 + n], bank[6][:, 0:n], ACT.Identity, bias=cols[:, 2:3]).then_inc(xu_done, 1)

            act.wait_ge(lane_done, 1)
            act.wait_ge(zeros_set, 3)
            act.wait_ge(base_done, 1)

            def squares(h, g2, k, edges=HALF):
                s, at = (k // 2) % 2, (k % 2) * HALF
                act.wait_ge(dist_loaded[s], g2 * 16 + 16)
                nc.scalar.activation(feat[0:RADIAL, s, at:at + HALF], dist_b[0:RADIAL, s, at:at + HALF],
                                     ACT.Square, bias=offset[0:RADIAL, :]).then_inc(square_done, 1)

            def gaussians(h, k):
                s, at = (k // 2) % 2, (k % 2) * HALF
                act.wait_ge(square_done, h + 1)
                nc.scalar.activation(feat[0:RADIAL, s, at:at + HALF], feat[0:RADIAL, s, at:at + HALF],
                                     ACT.Exp, scale=-0.5 / (CUTOFF / (RADIAL - 1)) ** 2).then_inc(radial_ready, 1)

            with act.If(is_fast(act) > 0):
                for h in (0, 1):
                    squares(h, 0, h)
                    gaussians(h, h)

                def step(h, g2_next, k):
                    if not isinstance(h, int) or h < H:
                        act.wait_ge(pre_done, h + 1)
                        if not isinstance(h, int) or h >= 2:
                            act.wait_ge(h1_ready, h - 1)
                        nc.scalar.activation(th1[:, k % 2, :], pre_ps[k % 2][:, :], ACT.Tanh, scale=0.5).then_inc(tanh1_done, 1)
                    if not isinstance(h, int) or h + 2 < H:
                        squares(h + 2, g2_next, (k + 2) % 4)
                    if not isinstance(h, int) or 1 <= h <= H:
                        act.wait_ge(l2_done, h)
                        if not isinstance(h, int) or h >= 3:
                            act.wait_ge(h2_ready, h - 2)
                        nc.scalar.activation(th2[:, (k - 1) % 2, :], l2_ps[(k - 1) % 2][:, :], ACT.Tanh, scale=0.5)\
                            .then_inc(tanh2_done, 1)
                    if not isinstance(h, int) or h + 2 < H:
                        gaussians(h + 2, (k + 2) % 4)

                for h in range(4):
                    step(h, (h + 2) // 4, h)
                with act.Fori(0, LOOPS) as i:
                    for k in range(4):
                        step(i * 4 + (4 + k), i + (1 + k // 2), k)
                for h in range(H - 2, H + 1):
                    step(h, (h + 2) // 4, h % 4)
            with act.Else():
                with act.Fori(0, G) as g:
                    act.wait_ge(gen_dist_loaded, g * 16 + 16)
                    nc.scalar.activation(feat[0:RADIAL, 0, :], dist_b[0:RADIAL, 0, :], ACT.Square,
                                         bias=offset[0:RADIAL, :]).then_inc(gen_square_done, 1)
                    act.wait_ge(gen_square_done, g + 1)
                    nc.scalar.activation(feat[0:RADIAL, 0, :], feat[0:RADIAL, 0, :], ACT.Exp,
                                         scale=-0.5 / (CUTOFF / (RADIAL - 1)) ** 2).then_inc(gen_radial_ready, 1)
                    with act.Fori(0, NW) as w:
                        act.wait_ge(gen_pre_done, g * NW + w + 1)
                        for s in range(2):
                            a = nc.scalar.activation(th1[:, s, :], pre_ps[s][:, :], ACT.Tanh, scale=0.5)
                        a.then_inc(gen_tanh1_done, 1)
                        act.wait_ge(gen_l2_done, g * NW + w + 1)
                        for s in range(2):
                            a = nc.scalar.activation(th2[:, s, :], l2_ps[s][:, :], ACT.Tanh, scale=0.5)
                        a.then_inc(gen_tanh2_done, 1)

            for c in range(NCH + 1):
                if c < NCH:
                    n0, n = chunk[c]
                    act.wait_ge(z1_done, c + 1)
                    nc.scalar.activation(s1[:, n0:n0 + n], xu[:, n0:n0 + n], ACT.Silu).then_inc(s1_done, 1)
                if c >= 1:
                    n0, n = chunk[c - 1]
                    act.wait_ge(b_ps, c)
                    nc.scalar.activation(s2[:, n0:n0 + n], bank[2 + (c - 1) % 2][:, 0:n], ACT.Silu, bias=bui[:, :])\
                        .then_inc(s2_done, 1)
            act.wait_ge(mv_done, NB)
            nc.scalar.activation(std[:, :], mv[:, :, 1], ACT.Sqrt, bias=eps[:, :]).then_inc(std_done, 1)

        @block.vector
        def _(dve):
            chain = [0]

            def link(ins):
                chain[0] += 1
                ins.then_inc(v_chain, 1)
                dve.wait_ge(v_chain, chain[0])

            nc.vector.memset(dst_i[:, :], FAR).then_inc(pads_set, 1)
            nc.vector.memset(src_i[:, :], 0).then_inc(pads_set, 1)
            nc.vector.memset(xn[:, NB - 1, :], 0.0).then_inc(zeros_set, 1)
            nc.vector.memset(left[32:WIN, :, :], 0.0).then_inc(zeros_set, 1)
            nc.vector.memset(feat[:, :, :], 0.0).then_inc(zeros_set, 1)
            nc.vector.memset(src_col[:, G, :], 0)
            nc.vector.memset(eps[:, :], EPS)
            nc.vector.memset(agg[:, :, :], 0.0).then_inc(agg_added, 1)

            dve.wait_ge(dst_loaded, 32)
            nc.vector.tensor_copy(dst_f[:, :], dst_i[:, :]).then_inc(v_chain, 1)
            chain[0] += 1
            dve.wait_ge(v_chain, chain[0])
            nc.vector.tensor_reduce(least[0:G, 0:1], dst_f[0:G, 0:REST], AX.X, ALU.min)
            nc.vector.tensor_reduce(least[0:FULL, 1:2], dst_f[0:FULL, REST:GROUP], AX.X, ALU.min)
            nc.vector.tensor_reduce(most[0:G, 0:1], dst_f[0:G, 0:REST], AX.X, ALU.max)
            link(nc.vector.tensor_reduce(most[0:FULL, 1:2], dst_f[0:FULL, REST:GROUP], AX.X, ALU.max))
            nc.vector.tensor_tensor(least[0:FULL, 0:1], least[0:FULL, 0:1], least[0:FULL, 1:2], ALU.min)
            link(nc.vector.tensor_tensor(most[0:FULL, 0:1], most[0:FULL, 0:1], most[0:FULL, 1:2], ALU.max))
            link(nc.vector.tensor_scalar(base[0:G, 0:1], least[0:G, 0:1], float(N - WIN), None, ALU.min))
            link(nc.vector.tensor_tensor(wide[0:G, 1:2], most[0:G, 0:1], base[0:G, 0:1], ALU.subtract))
            nc.vector.tensor_scalar(wide[0:G, 0:1], wide[0:G, 1:2], -1.0 if force_general else float(WIN), None, ALU.is_ge)\
                .then_inc(wide_done, 1)

            def store_pq(c):
                for b in chunk_blocks[c]:
                    dve.wait_ge(pq_ps_done, b + 1)
                    nc.vector.tensor_tensor(p_out[:, b, :], bank[2 + b % 4][:, 0:D], b1_all[:, :], ALU.add)
                    nc.vector.tensor_copy(q_out[:, b, :], bank[2 + b % 4][:, D:2 * D]).then_inc(pq_done, 1)

            dve.wait_ge(first_weights, 48)
            store_pq(0)
            store_pq(1)
            dve.wait_ge(wide_ps, 1)
            link(nc.vector.tensor_scalar(base[:, 2:3], bank[6][:, 0:1], 0.0, None, ALU.is_equal))
            nc.vector.tensor_copy(sorted_i[:, :], base[:, 2:3])
            link(nc.vector.tensor_tensor(base[0:G, 1:2], base[0:G, 0:1], base[0:G, 2:3], ALU.mult))
            nc.vector.tensor_copy(base_i[0:G, :], base[0:G, 1:2]).then_inc(base_done, 1)
            dve.wait_ge(edges_loaded, 32)
            nc.vector.tensor_copy(src_f[:, :], src_i[:, :])
            nc.vector.tensor_scalar(dst_f[0:G, :], dst_f[0:G, :], base[0:G, 1:2], None, ALU.subtract).then_inc(rel_done, 1)
            for c in range(2, NCH):
                store_pq(c)

            for n, col in enumerate((src_col, rel_col)):
                dve.wait_ge(tables_ps, n + 1)
                for q in range(2):
                    nc.vector.tensor_copy(col[:, 0:G, 4 * q:4 * q + 4],
                                          bank[6 + q][:, 0:4 * G].rearrange("p (j g) -> p g j", g=G)).then_inc(tables_done, 1)
            dve.wait_ge(tables_done, 4)

            def take_index(h, g, k):
                nc.vector.tensor_scalar(index[:, k, :], src_col[:, bass.ds(g, 1), (k % 2) * HT:(k % 2 + 1) * HT]
                                        .rearrange("p a t -> p (a t)"), 0.0, None, ALU.add).then_inc(index_ready, 1)

            with dve.If(is_fast(dve) > 0):
                for h in range(4):
                    take_index(h, h // 2, h)

            dve.wait_ge(pool_const, 6)
            link(nc.vector.tensor_copy(lane[:, :], lane_i[:, :]))
            nc.vector.tensor_copy(win[:, :], win_i[:, :])
            nc.vector.tensor_scalar(offset[:, :], lane[:, :], float(WIN), -CUTOFF / (RADIAL - 1), ALU.add, ALU.mult)\
                .then_inc(lane_done, 1)
            dve.wait_ge(b2_loaded, 16)
            link(nc.vector.tensor_copy(b2_part[:, 0, :], b2_row[:, :]))
            link(nc.vector.tensor_tensor(b2_left[:, 0, :], b2_row[:, :], b2_part[:, 0, :], ALU.subtract))
            link(nc.vector.tensor_copy(b2_part[:, 1, :], b2_left[:, 0, :]))
            link(nc.vector.tensor_tensor(b2_left[:, 1, :], b2_left[:, 0, :], b2_part[:, 1, :], ALU.subtract))
            nc.vector.tensor_copy(b2_part[:, 2, :], b2_left[:, 1, :]).then_inc(b2_loaded, 1)
            dve.wait_ge(weights_loaded, 16 * 14)
            nc.vector.tensor_scalar(w2half[:, :], w2[:, :], 0.5, None, ALU.mult)
            dve.wait_ge(turn_ps, 1)
            nc.vector.tensor_scalar(w3t[:, :], bank[6][:, 0:D], 0.5, None, ALU.mult).then_inc(turned, 1)
            nc.vector.tensor_copy(wu2t[:, :], bank[6][:, D:2 * D]).then_inc(turned, 1)
            dve.wait_ge(fold_ps, 1)
            nc.vector.tensor_copy(w3u[:, :], bank[7][:, 0:D])
            nc.vector.tensor_copy(wui[:, :], bank[7][:, D:2 * D])
            nc.vector.tensor_copy(b3u[:, :], bank[7][:, 2 * D:2 * D + 1])
            nc.vector.tensor_tensor(bui[:, :], bank[7][:, 2 * D + 1:2 * D + 2], cols[:, 3:4], ALU.add).then_inc(folded, 1)
            nc.vector.tensor_tensor(xn[:, :, :], xn[:, :, :],
                                    bi2_all[:, :].rearrange("p (a d) -> p a d", a=1).broadcast_to([P, NB, D]), ALU.add)\
                .then_inc(xb_done, 1)
            dve.wait_ge(base_loaded, 16)
            dve.wait_ge(xb_done, 1)

            def one_hot(h, g2, k):
                s, at = (k // 2) % 2, (k % 2) * HALF
                dve.wait_ge(rel_loaded[s], g2 * 16 + 16)
                nc.vector.tensor_scalar(feat[WIN:P, s, at:at + HALF], rel_b[WIN:P, s, at:at + HALF],
                                        lane[WIN:P, :], None, ALU.is_equal).then_inc(one_hot_ready, 1)

            def hot_edges(g, s):
                nc.vector.tensor_tensor(hot[:, s, :, :],
                                        win[:, :].rearrange("p (a w) -> p a w", a=1).broadcast_to([P, GT, WIN]),
                                        rel_col[:, bass.ds(g, 1), :].rearrange("p a t -> p (a t)")
                                        .rearrange("p (t a) -> p t a", a=1).broadcast_to([P, GT, WIN]),
                                        ALU.is_equal).then_inc(hot_ready, 1)

            def add_window(g, s):
                b = dve.value_load(base_sb[0:1, bass.ds(g, 1)], min_val=0, max_val=N - WIN)
                dve.wait_ge(agg_added, g + 1)
                at = agg[:, :, bass.ds(b, WIN)]
                nc.vector.tensor_tensor(at, at, agg_ps[s][:, 0:2 * WIN].rearrange("p (a w) -> p a w", a=2), ALU.add)\
                    .then_inc(agg_added, 1)

            with dve.If(is_fast(dve) > 0):
                for h in (0, 1):
                    one_hot(h, 0, h)

                def step(h, g, g2_next, k):
                    whole = not isinstance(h, int)
                    s = (k // 2) % 2
                    if whole or h < H:
                        dve.wait_ge(tanh1_done, h + 1)
                        if whole or h >= 2:
                            dve.wait_ge(l2_done, h - 1)
                        nc.vector.scalar_tensor_tensor(out=h1[:, k % 2, :], in0=th1[:, k % 2, :], scalar=1.0,
                                                       in1=pre_ps[k % 2][:, :], op0=ALU.add, op1=ALU.mult).then_inc(h1_ready, 1)
                    if whole or h + 4 < H:
                        take_index(h + 4, g + 2, k)
                    if whole or h + 2 < H:
                        one_hot(h + 2, g2_next, (k + 2) % 4)
                    if k % 2 == 0:
                        if whole or g >= 2:
                            dve.wait_ge(seg_done, h - 2)
                            add_window(g - 2, s)
                        if whole or g < G:
                            hot_edges(g, s)
                    if whole or 1 <= h <= H:
                        dve.wait_ge(tanh2_done, h)
                        if whole or h >= 3:
                            dve.wait_ge(seg_done, h - 2)
                        nc.vector.scalar_tensor_tensor(out=h2[:, (k - 1) % 2, :], in0=th2[:, (k - 1) % 2, :], scalar=1.0,
                                                       in1=l2_ps[(k - 1) % 2][:, :], op0=ALU.add, op1=ALU.mult)\
                            .then_inc(h2_ready, 1)

                for h in range(4):
                    step(h, h // 2, (h + 2) // 4, h)
                with dve.Fori(0, LOOPS) as i:
                    for k in range(4):
                        step(i * 4 + (4 + k), i * 2 + (2 + k // 2), i + (1 + k // 2), k)
                for h in range(H - 2, H + 1):
                    step(h, h // 2, (h + 2) // 4, h % 4)
                dve.wait_ge(seg_done, H)
                add_window(G - 1, (G - 1) % 2)
                dve.wait_ge(agg_added, G + 1)
            with dve.Else():
                nc.vector.memset(wide[:, :], 0.0).then_inc(gen_added, 1)
                with dve.Fori(0, G) as g:
                    dve.wait_ge(gen_added, g * NW + 1)
                    nc.vector.tensor_scalar(index[:, 0:2, :].rearrange("p s t -> p (s t)"),
                                            src_col[:, bass.ds(g, 1), :].rearrange("p a t -> p (a t)"), 0.0, None,
                                            ALU.add).then_inc(gen_index_ready, 1)
                    nc.vector.tensor_scalar(rel_col[:, G, :], rel_col[:, bass.ds(g, 1), :].rearrange("p a t -> p (a t)"),
                                            0.0, None, ALU.add).then_inc(gen_rel_ready, 1)
                    with dve.Fori(0, NW) as w:
                        dve.wait_ge(gen_rel_loaded, g * 16 + 16)
                        dve.wait_ge(gen_rel_ready, g * (NW + 1) + w + 1)
                        nc.vector.tensor_scalar(feat[WIN:P, 0, :], rel_b[WIN:P, 0, :], lane[WIN:P, :], None, ALU.is_equal)
                        nc.vector.tensor_tensor(hot[:, 0, :, :],
                                                win[:, :].rearrange("p (a w) -> p a w", a=1).broadcast_to([P, GT, WIN]),
                                                rel_col[:, G, :].rearrange("p (t a) -> p t a", a=1)
                                                .broadcast_to([P, GT, WIN]), ALU.is_equal).then_inc(gen_hot_ready, 1)
                        dve.wait_ge(gen_hot_ready, g * NW + w + 1)
                        nc.vector.tensor_scalar(rel_b[WIN:P, 0, :], rel_b[WIN:P, 0, :], float(WIN), None, ALU.subtract)
                        nc.vector.tensor_scalar(rel_col[:, G, :], rel_col[:, G, :], float(WIN), None, ALU.subtract)\
                            .then_inc(gen_rel_ready, 1)
                        dve.wait_ge(gen_tanh1_done, g * NW + w + 1)
                        for s in range(2):
                            m = nc.vector.scalar_tensor_tensor(out=h1[:, s, :], in0=th1[:, s, :], scalar=1.0,
                                                               in1=pre_ps[s][:, :], op0=ALU.add, op1=ALU.mult)
                        m.then_inc(gen_h1_ready, 1)
                        dve.wait_ge(gen_tanh2_done, g * NW + w + 1)
                        for s in range(2):
                            m = nc.vector.scalar_tensor_tensor(out=h2[:, s, :], in0=th2[:, s, :], scalar=1.0,
                                                               in1=l2_ps[s][:, :], op0=ALU.add, op1=ALU.mult)
                        m.then_inc(gen_h2_ready, 1)
                        dve.wait_ge(gen_seg_done, g * NW + w + 1)
                        at = agg[:, :, bass.ds(w * WIN, WIN)]
                        nc.vector.tensor_tensor(at, at, agg_ps[0][:, 0:2 * WIN].rearrange("p (a w) -> p a w", a=2),
                                                ALU.add).then_inc(gen_added, 1)
                dve.wait_ge(gen_added, G * NW + 1)
            nc.vector.memset(wide[:, :], 0.0).then_inc(edges_done, 1)

            for c in range(NCH + 2):
                if c < NCH:
                    n0, n = chunk[c]
                    if c == 0:
                        dve.wait_ge(folded, 1)
                        dve.wait_ge(xu_done, NCH)
                    nc.vector.scalar_tensor_tensor(out=xu[:, n0:n0 + n], in0=agg[:, 1, n0:n0 + n], scalar=b3u[:, :],
                                                   in1=xu[:, n0:n0 + n], op0=ALU.mult, op1=ALU.add).then_inc(deg_done, 1)
                    dve.wait_ge(a_ps, c + 1)
                    dve.wait_ge(deg_done, c + 1)
                    nc.vector.tensor_tensor(xu[:, n0:n0 + n], bank[c % 2][:, 0:n], xu[:, n0:n0 + n], ALU.add)\
                        .then_inc(z1_done, 1)
                if c >= 2:
                    bs = chunk_blocks[c - 2]
                    m = P if (c - 2) < NCH - 1 else min(P, NCOL - bs.start * P)
                    dve.wait_ge(c_ps, c - 1)
                    nc.vector.tensor_tensor(y[0:m, bs.start:bs.stop, :], xn[0:m, bs.start:bs.stop, :],
                                            bank[4 + c % 2][0:m, 0:len(bs) * D].rearrange("p (b d) -> p b d", d=D), ALU.add)\
                        .then_inc(y_done, 1)
                    dve.wait_ge(y_done, c - 1)
                    for b in bs:
                        m = min(P, NCOL - b * P)
                        if b == NB - 1:
                            link(nc.vector.memset(mv[:, b, :], 1.0))
                        nc.vector.bn_stats(stats[0:m, b, :], y[0:m, b, :]).then_inc(stats_done, 1)
                        dve.wait_ge(stats_done, b + 1)
                        nc.vector.bn_aggr(mv[0:m, b, :], stats[0:m, b, :]).then_inc(mv_done, 1)
            dve.wait_ge(std_done, 1)
            nc.vector.reciprocal(rstd[:, :], std[:, :]).then_inc(rstd_done, 1)
            dve.wait_ge(rstd_done, 1)
            for b in range(NB):
                m = min(P, NCOL - b * P)
                nc.vector.tensor_scalar(res[0:m, b, :], y[0:m, b, :], mv[0:m, b, 0:1], rstd[0:m, b:b + 1],
                                        ALU.subtract, ALU.mult).then_inc(res_done, 1)


_INS = ['x', 'src', 'dst', 'edge_weight', 'L0_gnn_Wm1', 'L0_gnn_bm1', 'L0_gnn_Wm2', 'L0_gnn_bm2', 'L0_gnn_Wm3',
        'L0_gnn_bm3', 'L0_gnn_Wu1', 'L0_gnn_bu1', 'L0_gnn_Wu2', 'L0_gnn_bu2', 'L0_gnn_Wi1', 'L0_gnn_bi1',
        'L0_gnn_Wi2', 'L0_gnn_bi2']
_OUT = ((3125, 128), 'float32')


def kernel(**inputs):
    import numpy as _np
    import concourse.bacc as _bacc
    from concourse import mybir as _mybir
    from concourse.bass_utils import run_bass_kernel_spmd as _run

    nc = _bacc.Bacc("TRN2", target_bir_lowering=False, num_devices=1)
    arrays, args = {}, []
    for name in _INS:
        a = _np.ascontiguousarray(inputs[name])
        arrays[f"in_{name}_dram"] = a
        args.append(nc.dram_tensor(f"in_{name}_dram", a.shape, _mybir.dt.from_np(a.dtype), kind="ExternalInput").ap())
    out = nc.dram_tensor("out_0_dram", _OUT[0], _mybir.dt.from_np(_np.dtype(_OUT[1])), kind="ExternalOutput").ap()
    gnn_kernel(nc, *args, out)
    r = _run(nc, [arrays], core_ids=[0])
    return r.results[0]["out_0_dram"]
```

```python
from contextlib import ExitStack

import concourse.bass as bass
from concourse import mybir

F32 = mybir.dt.float32
BF16 = mybir.dt.bfloat16
I32 = mybir.dt.int32
ALU = mybir.AluOpType
ACT = mybir.ActivationFunctionType
AX = mybir.AxisListType

P = 128
RADIAL = 50
CUTOFF = 10.0
EPS = 1e-5
WIN = 64
TILE = 128
HALF = 512
HT = HALF // TILE
GROUP = 2 * HALF
GT = GROUP // TILE
SLOTS = 8
FAR = 8191


def gnn_kernel(nc, x, src, dst, dist, Wm1, bm1, Wm2, bm2, Wm3, bm3, Wu1, bu1, Wu2, bu2, Wi1, bi1,
               Wi2, bi2, out, force_general=False):
    N, D = x.shape
    E = src.shape[0]
    assert D == P
    NB = -(-N // P)
    NPAD = NB * P
    NW = -(-N // WIN)
    NCOL = NW * WIN
    G = -(-E // GROUP)
    H = 2 * G
    FULL = E // GROUP
    REST = E - FULL * GROUP
    assert G == FULL + 1 and G % 4 == 1 and G >= 9 and G <= P
    LOOPS = (H - 10) // SLOTS
    LASTN = N - (NB - 1) * P
    NCH = -(-NCOL // HALF)
    chunk = [(HALF * c, min(HALF, NCOL - HALF * c)) for c in range(NCH)]
    chunk_blocks = [range(4 * c, min(4 * c + 4, NB)) for c in range(NCH)]

    with ExitStack() as ctx:
        def sb(name, shape, dt=F32):
            return ctx.enter_context(nc.sbuf_tensor(name, shape, dt))

        def sem(name):
            return ctx.enter_context(nc.semaphore(name))

        p_rows = nc.dram_tensor("p_rows", (NPAD, D), F32).ap()
        q_rows = nc.dram_tensor("q_rows", (NPAD, D), F32).ap()
        rel_rows = nc.dram_tensor("rel_rows", (G, GROUP), F32).ap()
        base_row = nc.dram_tensor("base_row", (1, G), I32).ap()

        bank = [ctx.enter_context(nc.psum_tensor(f"bank{n}", [P, HALF], F32)) for n in range(8)]
        pre_ps, l2_ps, agg_ps = bank[0:2], bank[2:4], bank[4:6]

        w1a = sb("w1a", [P, D])
        w1b = sb("w1b", [P, D])
        w2 = sb("w2", [P, D])
        w2half = sb("w2half", [P, D])
        w3 = sb("w3", [P, D])
        w3t = sb("w3t", [P, D])
        wu1a = sb("wu1a", [P, D])
        wu1b = sb("wu1b", [P, D])
        wu2 = sb("wu2", [P, D])
        wu2t = sb("wu2t", [P, D])
        wi1 = sb("wi1", [P, D])
        wi2 = sb("wi2", [P, D])
        w3u = sb("w3u", [P, D])
        wui = sb("wui", [P, D])
        bi2_all = sb("bi2_all", [P, D])
        wi2c = sb("wi2c", [P, D])
        wi2_mean = sb("wi2_mean", [P, 1])
        cols = sb("cols", [P, 4])
        b3u = sb("b3u", [P, 1])
        bui = sb("bui", [P, 1])
        b2_row = sb("b2_row", [1, D])
        b2_part = sb("b2_part", [1, 3, D], BF16)
        b2_left = sb("b2_left", [1, 2, D])
        b2_rhs = sb("b2_rhs", [3, HT, D], BF16)
        ones_bf = sb("ones_bf", [P, P], BF16)
        ones_f = sb("ones_f", [P, P])
        ident = sb("ident", [P, P])
        lane = sb("lane", [P, 1])
        lane_i = sb("lane_i", [P, 1], I32)
        offset = sb("offset", [P, 1])
        win_i = sb("win_i", [P, WIN], I32)
        win = sb("win", [P, WIN])
        eps = sb("eps", [P, 1])

        xn = sb("xn", [P, NB, D])
        xt = sb("xt", [P, NPAD])
        y = xt[:, :].rearrange("p (b d) -> p b d", d=D)
        p_out = sb("p_out", [P, NB, D])
        q_out = sb("q_out", [P, NB, D])
        s1 = p_out[:, :, :].rearrange("p b d -> p (b d)")
        s2 = q_out[:, :, :].rearrange("p b d -> p (b d)")
        z = sb("z", [P, NPAD])
        xb_mean = sb("xb_mean", [P, NB])
        xg = sb("xg", [P, HALF])
        win_sum = sb("win_sum", [P, 2, WIN])

        src_i = sb("src_i", [P, GROUP], I32)
        dst_i = sb("dst_i", [P, GROUP], I32)
        src_f = sb("src_f", [P, GROUP])
        dst_f = sb("dst_f", [P, GROUP])
        least = sb("least", [P, 2])
        most = sb("most", [P, 2])
        base = sb("base", [P, 3])
        base_i = sb("base_i", [P, 1], I32)
        wide = sb("wide", [P, 2])
        sorted_i = sb("sorted_i", [P, 1], I32)
        base_sb = sb("base_sb", [1, G], I32)
        src_col = sb("src_col", [P, G + 3, GT], I32)
        rel_col = sb("rel_col", [P, G + 1, GT])

        index = sb("index", [P, SLOTS, HT], I32)
        rows = sb("rows", [P, SLOTS, HT, D])
        dist_b = sb("dist_b", [WIN, 2, GROUP])
        rel_b = sb("rel_b", [P, 2, GROUP])
        feat = sb("feat", [P, 2, GROUP])
        left = sb("left", [P, 2, D])
        hot = sb("hot", [P, 2, GT, WIN])
        th1 = sb("th1", [P, 2, HALF])
        h1 = sb("h1", [P, 2, HALF])
        th2 = sb("th2", [P, 2, HALF])
        h2 = sb("h2", [P, 2, HALF])
        y2 = sb("y2", [P, 2, HALF])
        var = sb("var", [P, NB])
        std = sb("std", [P, NB])
        rstd = sb("rstd", [P, NB])
        res = p_out

        x_loaded = [sem(f"x_loaded{n}") for n in range(3)]
        first_index = sem("first_index")
        weights_loaded = sem("weights_loaded")
        edges_loaded = sem("edges_loaded")
        dst_loaded = sem("dst_loaded")
        b2_loaded = sem("b2_loaded")
        b2_placed = sem("b2_placed")
        pool_const = sem("pool_const")
        pads_set = sem("pads_set")
        zeros_set = sem("zeros_set")
        v_chain = sem("v_chain")
        src_done = sem("src_done")
        src_ps = sem("src_ps")
        src_col_done = sem("src_col_done")
        xt_ps_done = sem("xt_ps_done")
        xt_done = sem("xt_done")
        p_ps = sem("p_ps")
        p_done = sem("p_done")
        q_ps = sem("q_ps")
        q_done = sem("q_done")
        w1a_loaded = sem("w1a_loaded")
        w1b_loaded = sem("w1b_loaded")
        p_stored = sem("p_stored")
        q_stored = sem("q_stored")
        tables_ps = sem("tables_ps")
        tables_done = sem("tables_done")
        wide_done = sem("wide_done")
        wide_ps = sem("wide_ps")
        base_done = sem("base_done")
        rel_done = sem("rel_done")
        rel_stored = sem("rel_stored")
        base_stored = sem("base_stored")
        base_loaded = sem("base_loaded")
        turn_ps = sem("turn_ps")
        turned = sem("turned")
        fold_ps = sem("fold_ps")
        folded = sem("folded")
        xu_ps = sem("xu_ps")
        xu_done = sem("xu_done")
        lane_done = sem("lane_done")
        index_ready = sem("index_ready")
        index_seen = sem("index_seen")
        gathered = [sem(f"gathered{n}") for n in range(SLOTS)]
        dist_loaded = [sem(f"dist_loaded{n}") for n in range(2)]
        rel_loaded = [sem(f"rel_loaded{n}") for n in range(2)]
        q_loaded = [sem(f"q_loaded{n}") for n in range(2)]
        square_done = sem("square_done")
        radial_ready = sem("radial_ready")
        one_hot_ready = sem("one_hot_ready")
        pre_done = sem("pre_done")
        tanh1_done = sem("tanh1_done")
        h1_ready = sem("h1_ready")
        l2_done = sem("l2_done")
        tanh2_done = sem("tanh2_done")
        h2_ready = sem("h2_ready")
        hot_ready = sem("hot_ready")
        seg_done = sem("seg_done")
        xg_ps = sem("xg_ps")
        xg_ready = sem("xg_ready")
        win_ready = sem("win_ready")
        win_ps = sem("win_ps")
        z_added = sem("z_added")
        gen_added = sem("gen_added")
        gen_index_ready = sem("gen_index_ready")
        gen_gathered = sem("gen_gathered")
        gen_dist_loaded = sem("gen_dist_loaded")
        gen_square_done = sem("gen_square_done")
        gen_radial_ready = sem("gen_radial_ready")
        gen_rel_loaded = sem("gen_rel_loaded")
        gen_rel_ready = sem("gen_rel_ready")
        gen_q_loaded = sem("gen_q_loaded")
        gen_hot_ready = sem("gen_hot_ready")
        gen_pre_done = sem("gen_pre_done")
        gen_tanh1_done = sem("gen_tanh1_done")
        gen_h1_ready = sem("gen_h1_ready")
        gen_l2_done = sem("gen_l2_done")
        gen_tanh2_done = sem("gen_tanh2_done")
        gen_h2_ready = sem("gen_h2_ready")
        gen_seg_done = sem("gen_seg_done")
        gen_win_ready = sem("gen_win_ready")
        gen_win_ps = sem("gen_win_ps")
        edges_done = sem("edges_done")
        s1_done = sem("s1_done")
        b_ps = sem("b_ps")
        s2_done = sem("s2_done")
        c_ps = sem("c_ps")
        y_done = sem("y_done")
        y2_done = sem("y2_done")
        var_done = sem("var_done")
        std_done = sem("std_done")
        rstd_done = sem("rstd_done")
        res_done = sem("res_done")
        out_stored = sem("out_stored")
        xb_done = sem("xb_done")
        wi2_done = sem("wi2_done")

        block = ctx.enter_context(nc.Block())
        LASTT = -(-(REST - HALF) // TILE) if REST > HALF else 1
        XA, XB = 4, 12
        dst_whole = dst[0:FULL * GROUP].rearrange("(g e) -> g e", e=GROUP)
        src_whole = src[0:FULL * GROUP].rearrange("(g e) -> g e", e=GROUP)
        dst_rest = dst[FULL * GROUP:E].rearrange("(a e) -> a e", a=1)
        src_rest = src[FULL * GROUP:E].rearrange("(a e) -> a e", a=1)
        dist_row = dist.rearrange("(a e) -> a e", a=1)

        def loops(h):
            return not isinstance(h, int)

        def later(h, first):
            return loops(h) or h >= first

        def early(h):
            return not loops(h) and h < 4

        def half_edges(h):
            return LASTT * TILE if not loops(h) and h == H - 1 else HALF

        def row_of(v):
            return v.rearrange("(a d) -> a d", a=1)

        def col_of(v):
            return v.rearrange("(d a) -> d a", a=1)

        def is_fast(eng):
            return eng.value_load(sorted_i[0:1, 0:1], min_val=0, max_val=1)

        @block.sync
        def _(sp):
            sp.dma_start(index[:, 0:4, :].rearrange("p s t -> p (s t)"),
                         src[0:4 * HALF].rearrange("(c p) -> p c", p=P), allow_slow_non_contiguous=True).then_inc(first_index, 16)
            sp.dma_start(xn[:, 0:XA, :], x[0:XA * P, :].rearrange("(b p) d -> p b d", p=P)).then_inc(x_loaded[0], 16)
            sp.dma_start(xn[:, XA:XB, :], x[XA * P:XB * P, :].rearrange("(b p) d -> p b d", p=P)).then_inc(x_loaded[1], 16)
            sp.dma_start(xn[:, XB:NB - 1, :],
                         x[XB * P:(NB - 1) * P, :].rearrange("(b p) d -> p b d", p=P)).then_inc(x_loaded[2], 16)
            sp.wait_ge(pads_set, 3)
            sp.dma_start(xn[0:LASTN, NB - 1, :], x[(NB - 1) * P:N, :]).then_inc(x_loaded[2], 16)
            sp.wait_ge(zeros_set, 1)
            sp.dma_start(left[0:RADIAL, 0, :], Wm1[2 * D:2 * D + RADIAL, :]).then_inc(weights_loaded, 16)
            sp.dma_start(left[0:RADIAL, 1, :], Wm1[2 * D:2 * D + RADIAL, :]).then_inc(weights_loaded, 16)
            for s in range(2):
                sp.dma_start(left[RADIAL:RADIAL + 1, s, :], row_of(bm1)).then_inc(weights_loaded, 16)
            for tile_, dram in ((w2, Wm2), (w3, Wm3), (wu1a, Wu1[0:D, :]), (wu1b, Wu1[D:2 * D, :]),
                                (wu2, Wu2), (wi1, Wi1), (wi2, Wi2),
                                (bi2_all, row_of(bi2).broadcast_to([P, D]))):
                sp.dma_start(tile_[:, :], dram).then_inc(weights_loaded, 16)
            for n, v in enumerate((bm3, bu2, bu1, bi1)):
                sp.dma_start(cols[:, n:n + 1], col_of(v)).then_inc(weights_loaded, 16)

            def load_dist(g, s, edges=GROUP):
                sp.dma_start(dist_b[:, s, 0:edges],
                             dist_row[:, bass.ds(g * GROUP, edges)].broadcast_to([WIN, edges])).then_inc(dist_loaded[s], 16)

            def load_rel(g, s):
                sp.dma_start(rel_b[WIN:P, s, :],
                             rel_rows[bass.ds(g, 1), :].broadcast_to([WIN, GROUP])).then_inc(rel_loaded[s], 16)

            for g in range(2):
                load_dist(g, g)

            def store_rows(c, done, made, rows_out, stored):
                bs = slice(chunk_blocks[c].start, chunk_blocks[c].stop)
                sp.wait_ge(done, c + 1)
                sp.dma_start(rows_out[bs.start * P:bs.stop * P, :].rearrange("(b p) d -> p b d", p=P), made[:, bs, :])\
                    .then_inc(stored, 16)

            for c in range(NCH):
                store_rows(c, p_done, p_out, p_rows, p_stored)
                if c == 1:
                    sp.wait_ge(base_done, 1)
                    sp.dma_start(base_row.rearrange("a g -> g a"), base_i[0:G, :]).then_inc(base_stored, 16)
                    sp.wait_ge(rel_done, 1)
                    sp.dma_start(rel_rows, dst_f[0:G, :]).then_inc(rel_stored, 16)
                if c == 3:
                    sp.wait_ge(base_stored, 16)
                    sp.dma_start(base_sb[:, :], base_row).then_inc(base_loaded, 16)
            sp.wait_ge(rel_stored, 16)
            for g in range(2):
                load_rel(g, g)
            sp.wait_ge(b2_loaded, 17)
            for n in range(3):
                sp.dma_start(b2_rhs[n:n + 1, :, :],
                             b2_part[:, n:n + 1, :].broadcast_to([1, HT, D])).then_inc(b2_placed, 16)
            for c in range(NCH):
                store_rows(c, q_done, q_out, q_rows, q_stored)
            sp.wait_ge(base_loaded, 16)

            def load_q(b, s):
                sp.dma_start(left[WIN:P, s, :], q_rows[bass.ds(b, WIN), :]).then_inc(q_loaded[s], 16)

            def group_base(g):
                return sp.value_load(base_sb[0:1, bass.ds(g, 1)], min_val=0, max_val=N - WIN)

            def load_group(g, s, g_before, edges=GROUP):
                b = group_base(g)
                sp.wait_ge(square_done, g_before)
                load_dist(g, s, edges)
                sp.wait_ge(one_hot_ready, g_before)
                load_rel(g, s)
                sp.wait_ge(pre_done, g_before)
                load_q(b, s)

            def general_loads(g, edges):
                sp.wait_ge(gen_added, g * NW + 1)
                sp.dma_start(dist_b[:, 0, 0:edges], dist_row[:, bass.ds(g * GROUP, edges)].broadcast_to([WIN, edges]))\
                    .then_inc(gen_dist_loaded, 16)
                sp.dma_start(rel_b[WIN:P, 0, :], rel_rows[bass.ds(g, 1), :].broadcast_to([WIN, GROUP]))\
                    .then_inc(gen_rel_loaded, 16)
                with sp.Fori(0, NW) as w:
                    sp.wait_ge(gen_added, w + (g * NW + 1))
                    sp.dma_start(left[WIN:P, 0, :], q_rows[bass.ds(w * WIN, WIN), :]).then_inc(gen_q_loaded, 16)

            with sp.If(is_fast(sp) > 0):
                bases = [group_base(g) for g in range(2)]
                sp.wait_ge(q_stored, 16 * NCH)
                for g in range(2):
                    load_q(bases[g], g)
                with sp.Fori(0, (G - 3) // 2) as i:
                    load_group(i * 2 + 2, 0, i * 4 + 2)
                    load_group(i * 2 + 3, 1, i * 4 + 4)
                load_group(G - 1, (G - 1) % 2, 2 * (G - 1) - 2, REST)
            with sp.Else():
                sp.wait_ge(q_stored, 16 * NCH)
                sp.wait_ge(square_done, 2)
                for n in range(2):
                    sp.wait_ge(rel_loaded[n], 16)
                with sp.Fori(0, FULL) as g:
                    general_loads(g, GROUP)
                general_loads(FULL, REST)

            for c in range(NCH):
                bs = chunk_blocks[c]
                sp.wait_ge(res_done, c + 1)
                whole = min(bs.stop, NB - 1)
                if whole > bs.start:
                    sp.dma_start(out[bs.start * P:whole * P, :].rearrange("(b p) d -> p b d", p=P),
                                 res[:, bs.start:whole, :]).then_inc(out_stored, 16)
            sp.dma_start(out[(NB - 1) * P:N, :], res[0:LASTN, NB - 1, :]).then_inc(out_stored, 16)
            sp.wait_ge(out_stored, 16 * ((NB - 1 + 3) // 4 + 1))

        @block.gpsimd
        def _(pool):
            nc.gpsimd.memset(ident[:, :], 0.0).then_inc(pool_const, 1)
            pool.wait_ge(pool_const, 1)
            nc.gpsimd.affine_select(out=ident[:, :], in_=ident[:, :], compare_op=ALU.not_equal, fill=1.0,
                                    base=0, pattern=[[-1, P]], channel_multiplier=1).then_inc(pool_const, 1)
            nc.gpsimd.iota(lane_i[:, :], pattern=[[0, 1]], base=-WIN, channel_multiplier=1).then_inc(pool_const, 1)
            nc.gpsimd.iota(win_i[:, :], pattern=[[1, WIN]], base=0, channel_multiplier=0).then_inc(pool_const, 1)
            nc.gpsimd.memset(ones_bf[:, :], 1.0).then_inc(pool_const, 1)
            nc.gpsimd.memset(ones_f[:, :], 1.0).then_inc(pool_const, 1)
            def gather(h, s, table=p_rows, tiles=HT):
                if early(h):
                    pool.wait_ge(first_index, 16)
                else:
                    pool.wait_ge(index_ready, h + 1)
                pool.sem_inc(index_seen, 1)
                for j in range(tiles):
                    nc.gpsimd.indirect_dma_start(
                        rows[:, s, j, :], None, table,
                        bass.IndirectOffsetOnAxis(ap=index[:, s, j:j + 1], axis=0)).then_inc(gathered[s], 16)

            for h in range(4):
                gather(h, h, x)
            pool.wait_ge(p_stored, 16 * NCH)
            for h in range(4, 8):
                gather(h, h)
            pool.wait_ge(base_done, 1)
            with pool.If(is_fast(pool) > 0):
                with pool.Fori(0, LOOPS) as i:
                    for k in range(SLOTS):
                        gather(i * SLOTS + (8 + k), k)
                gather(H - 2, (H - 2) % SLOTS)
                gather(H - 1, (H - 1) % SLOTS, tiles=LASTT)
            with pool.Else():
                with pool.Fori(0, G) as g:
                    pool.wait_ge(gen_index_ready, g + 1)
                    pool.sem_inc(index_seen, 1)
                    for s in range(2):
                        for j in range(HT):
                            nc.gpsimd.indirect_dma_start(
                                rows[:, s, j, :], None, p_rows,
                                bass.IndirectOffsetOnAxis(ap=index[:, s, j:j + 1], axis=0)).then_inc(gen_gathered, 16)

            for c in range(NCH):
                bs = chunk_blocks[c]
                m = min(P, NCOL - bs.start * P)
                pool.wait_ge(y_done, c + 1)
                if c >= 2:
                    pool.wait_ge(var_done, c - 1)
                yc = y[0:m, bs.start:bs.stop, :]
                nc.gpsimd.tensor_tensor(y2[0:m, c % 2, 0:len(bs) * D].rearrange("p (b d) -> p b d", d=D), yc, yc, ALU.mult)\
                    .then_inc(y2_done, 1)

        @block.tensor
        def _(pe):
            pe.wait_ge(pool_const, 2)
            def turn_table(table, ps, done, read=None):
                for j in range(GT):
                    mm = nc.tensor.transpose(bank[6 + j // 4][:, (j % 4) * G:(j % 4 + 1) * G],
                                             table[0:G, j * TILE:(j + 1) * TILE], ident[0:G, 0:G])
                mm.then_inc(ps, 1)

            def turn_x(c):
                bs = chunk_blocks[c]
                if c >= 2:
                    pe.wait_ge(xt_done, c - 1)
                for b in bs:
                    if b == 0:
                        pe.wait_ge(x_loaded[0], 16)
                    if b == XA:
                        pe.wait_ge(x_loaded[1], 16)
                    if b == XB:
                        pe.wait_ge(x_loaded[2], 32)
                    mm = nc.tensor.transpose(bank[c % 2][:, (b - bs.start) * P:(b - bs.start + 1) * P],
                                             xn[:, b, :], ident[:, :])
                mm.then_inc(xt_ps_done, 1)

            def times_x(c, w, banks, ps, done):
                if c >= 2:
                    pe.wait_ge(done, c - 1)
                for n, b in enumerate(chunk_blocks[c]):
                    mm = nc.tensor.matmul(banks[c % 2][:, n * D:(n + 1) * D], xt[:, b * P:(b + 1) * P], w[:, :],
                                          start=True, stop=True)
                mm.then_inc(ps, 1)

            turn_x(0)
            pe.wait_ge(w1a_loaded, 16)
            for c in range(NCH):
                if c + 1 < NCH:
                    turn_x(c + 1)
                pe.wait_ge(xt_done, c + 1)
                times_x(c, w1a, bank[2:4], p_ps, p_done)
                if c == 2:
                    pe.wait_ge(pool_const, 6)
                    pe.wait_ge(wide_done, 1)
                    nc.tensor.matmul(bank[4][:, 0:1], ones_f[0:G, :], wide[0:G, 0:1], start=True, stop=True).then_inc(wide_ps, 1)
            pe.wait_ge(src_done, 1)
            turn_table(src_f, src_ps, src_col_done)
            pe.wait_ge(w1b_loaded, 16)
            pe.wait_ge(base_done, 1)
            for c in range(NCH):
                times_x(c, w1b, bank[4:6], q_ps, q_done)
                if c == 3:
                    pe.wait_ge(src_col_done, 2)
                    pe.wait_ge(rel_done, 1)
                    turn_table(dst_f, tables_ps, tables_done)

            def turn_weights():
                pe.wait_ge(weights_loaded, 16 * 16)
                nc.tensor.transpose(bank[7][:, 0:D], w3[:, :], ident[:, :])
                nc.tensor.transpose(bank[7][:, D:2 * D], wu2[:, :], ident[:, :]).then_inc(turn_ps, 1)

            def fold_weights():
                pe.wait_ge(turned, 2)
                nc.tensor.matmul(bank[7][:, 0:D], w3t[:, :], wu1b[:, :], start=True, stop=True)
                nc.tensor.matmul(bank[7][:, D:2 * D], wu2t[:, :], wi1[:, :], start=True, stop=True)
                nc.tensor.matmul(bank[7][:, 2 * D:2 * D + 1], wu1b[:, :], cols[:, 0:1], start=True, stop=True)
                nc.tensor.matmul(bank[7][:, 2 * D + 1:2 * D + 2], wi1[:, :], cols[:, 1:2], start=True, stop=True).then_inc(fold_ps, 1)

            def update_x(c):
                n0, n = chunk[c]
                if c < 2:
                    pe.wait_ge(q_done, NCH if c % 2 == (NCH - 1) % 2 else NCH - 1)
                else:
                    pe.wait_ge(xu_done, c - 1)
                nc.tensor.matmul(bank[4 + c % 2][:, 0:n], wu1a[:, :], xt[:, n0:n0 + n], start=True, stop=True)\
                    .then_inc(xu_ps, 1)

            pe.wait_ge(tables_done, 2)
            turn_weights()
            for c in range(NCH):
                update_x(c)
                if c == 2:
                    fold_weights()


            def turn_rows(h):
                pe.wait_ge(gathered[h], 16 * HT)
                for j in range(HT):
                    mm = nc.tensor.transpose(bank[6][:, j * TILE:(j + 1) * TILE], rows[:, h, j, :], ident[:, :])
                mm.then_inc(xg_ps, 1)

            def first_layer(h, g2, g4, k):
                s, at, n = (k // 2) % 2, (k % 2) * HALF, half_edges(h)
                if early(h):
                    turn_rows(h)
                pe.wait_ge(radial_ready, h + 1)
                pe.wait_ge(one_hot_ready, h + 1)
                if k % 2 == 0:
                    pe.wait_ge(q_loaded[s], g2 * 16 + 16)
                if later(h, 2):
                    pe.wait_ge(h1_ready, h - 1)
                nc.tensor.matmul(pre_ps[k % 2][:, 0:n], left[:, s, :], feat[:, s, at:at + n], start=True, stop=True)
                if early(h):
                    pe.wait_ge(xg_ready, h + 1)
                    mm = nc.tensor.matmul(pre_ps[k % 2][:, :], w1a[:, :], xg[:, :], start=False, stop=True,
                                          skip_group_check=True)
                else:
                    pe.wait_ge(gathered[k], g4 * (16 * HT) + 16 * (n // TILE))
                    for j in range(n // TILE):
                        mm = nc.tensor.matmul(pre_ps[k % 2][:, j * TILE:(j + 1) * TILE], rows[:, k, j, :], ident[:, :],
                                              start=False, stop=True, skip_group_check=True)
                mm.then_inc(pre_done, 1)

            def second_tiles(k, tiles):
                nc.tensor.matmul(l2_ps[k][:, 0:tiles * D], ones_bf[0:3, :],
                                 b2_rhs[:, 0:tiles, :].rearrange("p t d -> p (t d)"), start=True, stop=True)
                for j in range(tiles):
                    mm = nc.tensor.matmul(l2_ps[k][:, j * D:(j + 1) * D], h1[:, k, j * TILE:(j + 1) * TILE],
                                          w2half[:, :], start=False, stop=True, skip_group_check=True)
                return mm

            def second_layer(h, k):
                pe.wait_ge(h1_ready, h + 1)
                if not loops(h) and h == 0:
                    pe.wait_ge(b2_placed, 48)
                if later(h, 2):
                    pe.wait_ge(h2_ready, h - 1)
                second_tiles(k % 2, half_edges(h) // TILE).then_inc(l2_done, 1)

            def sum_tile(s, h2_tile, t, last):
                nc.tensor.matmul(agg_ps[s][:, 0:WIN], h2_tile, hot[:, s, t, :],
                                 start=t == 0, stop=t == last, skip_group_check=True)
                return nc.tensor.matmul(agg_ps[s][:, WIN:2 * WIN], ones_bf[:, :],
                                        hot[:, s, t, :].bitcast(BF16)[:, 1:2 * WIN:2],
                                        start=False, stop=t == last, skip_group_check=True)

            def sum_over_dst(h, g, k):
                s, tiles = (k // 2) % 2, half_edges(h) // TILE
                pe.wait_ge(h2_ready, h + 1)
                if k % 2 == 0:
                    pe.wait_ge(hot_ready, g + 1)
                    if later(g, 2):
                        pe.wait_ge(z_added, g * 2 - 3)
                for j in range(tiles):
                    t = (k % 2) * HT + j
                    mm = sum_tile(s, h2[:, k % 2, j * D:(j + 1) * D], t, (k % 2) * HT + tiles - 1 if k % 2 else -1)
                mm.then_inc(seg_done, 1)

            def window_product(g, s):
                pe.wait_ge(win_ready, g + 1)
                if later(g, 2):
                    pe.wait_ge(z_added, g * 2 - 1)
                nc.tensor.matmul(bank[6 + s][:, 0:WIN], w3u[:, :], win_sum[:, s, :], start=True, stop=True)\
                    .then_inc(win_ps, 1)

            def step(h, g, g2, g4, k):
                if loops(h) or h < H:
                    first_layer(h, g2, g4, k)
                if loops(h) or 1 <= h <= H:
                    second_layer(h - 1, (k - 1) % SLOTS)
                if k % 2 == 1 and later(h, 5):
                    window_product(g - 2, (k // 2) % 2)
                if loops(h) or 2 <= h <= H + 1:
                    sum_over_dst(h - 2, g - 1, (k - 2) % SLOTS)

            with pe.If(is_fast(pe) > 0):
                for h in range(8):
                    if h == 2:
                        pe.wait_ge(xu_done, NCH)
                    step(h, h // 2, h // 4, 0, h)
                with pe.Fori(0, LOOPS) as i:
                    for k in range(SLOTS):
                        step(i * 8 + (8 + k), i * 4 + (4 + k // 2), i * 2 + (2 + k // 4), i + 1, k)
                for h in range(H - 2, H + 2):
                    step(h, h // 2, h // 4, h // 8, h % 8)
                window_product(G - 1, (G - 1) % 2)
            with pe.Else():
                pe.wait_ge(xu_done, NCH)
                pe.wait_ge(folded, 1)
                pe.wait_ge(b2_placed, 48)
                with pe.Fori(0, G) as g:
                    with pe.Fori(0, NW) as w:
                        pe.wait_ge(gen_gathered, g * (16 * GT) + 16 * GT)
                        pe.wait_ge(gen_radial_ready, g + 1)
                        pe.wait_ge(gen_q_loaded, (g * NW + w + 1) * 16)
                        pe.wait_ge(gen_hot_ready, g * NW + w + 1)
                        for s in range(2):
                            nc.tensor.matmul(pre_ps[s][:, :], left[:, 0, :], feat[:, 0, s * HALF:(s + 1) * HALF],
                                             start=True, stop=True)
                            for j in range(HT):
                                mm = nc.tensor.matmul(pre_ps[s][:, j * TILE:(j + 1) * TILE], rows[:, s, j, :],
                                                      ident[:, :], start=False, stop=True, skip_group_check=True)
                        mm.then_inc(gen_pre_done, 1)
                        pe.wait_ge(gen_h1_ready, g * NW + w + 1)
                        for s in range(2):
                            mm = second_tiles(s, HT)
                        mm.then_inc(gen_l2_done, 1)
                        pe.wait_ge(gen_h2_ready, g * NW + w + 1)
                        for t in range(GT):
                            mm = sum_tile(0, h2[:, t // HT, t % HT * D:(t % HT + 1) * D], t, GT - 1)
                        mm.then_inc(gen_seg_done, 1)
                        pe.wait_ge(gen_win_ready, g * NW + w + 1)
                        nc.tensor.matmul(bank[6][:, 0:WIN], w3u[:, :], win_sum[:, 0, :], start=True, stop=True)\
                            .then_inc(gen_win_ps, 1)

            def update_b(c):
                n0, n = chunk[c]
                pe.wait_ge(s1_done, c + 1)
                if c >= 2:
                    pe.wait_ge(s2_done, c - 1)
                nc.tensor.matmul(bank[c % 2][:, 0:n], wui[:, :], s1[:, n0:n0 + n], start=True, stop=True).then_inc(b_ps, 1)

            def update_c(c):
                pe.wait_ge(s2_done, c + 1)
                if c >= 2:
                    pe.wait_ge(y_done, c - 1)
                for n, b in enumerate(chunk_blocks[c]):
                    m = min(P, NCOL - b * P)
                    mm = nc.tensor.matmul(bank[2 + c % 2][0:m, n * D:(n + 1) * D], s2[:, b * P:b * P + m], wi2c[:, :],
                                          start=True, stop=True)
                mm.then_inc(c_ps, 1)

            pe.wait_ge(edges_done, 1)
            pe.wait_ge(wi2_done, 1)
            for c in range(NCH + 1):
                if c < NCH:
                    update_b(c)
                if c >= 1:
                    update_c(c - 1)

        @block.scalar
        def _(act):
            act.wait_ge(pads_set, 1)
            act.dma_start(dst_i[0:FULL, :], dst_whole).then_inc(dst_loaded, 16)
            act.dma_start(dst_i[FULL:G, 0:REST], dst_rest).then_inc(dst_loaded, 16)
            act.dma_start(w1a[:, :], Wm1[0:D, :]).then_inc(w1a_loaded, 16)
            act.wait_ge(pads_set, 2)
            act.dma_start(src_i[0:FULL, :], src_whole).then_inc(edges_loaded, 16)
            act.dma_start(src_i[FULL:G, 0:REST], src_rest).then_inc(edges_loaded, 16)
            act.dma_start(w1b[:, :], Wm1[D:2 * D, :]).then_inc(w1b_loaded, 16)
            act.dma_start(b2_row[:, :], row_of(bm2)).then_inc(b2_loaded, 16)
            act.wait_ge(pool_const, 3)
            nc.scalar.activation(lane[:, :], lane_i[:, :], ACT.Copy).then_inc(lane_done, 1)
            for c in range(NCH):
                n = len(chunk_blocks[c]) * P
                act.wait_ge(xt_ps_done, c + 1)
                nc.scalar.activation(xt[:, c * HALF:c * HALF + n], bank[c % 2][:, 0:n], ACT.Copy).then_inc(xt_done, 1)
                if c == 2:
                    act.wait_ge(edges_loaded, 32)
                    nc.scalar.activation(src_f[0:G, :], src_i[0:G, :], ACT.Copy).then_inc(src_done, 1)
            act.wait_ge(src_ps, 1)
            for q in range(2):
                nc.scalar.activation(src_col[:, 0:G, 4 * q:4 * q + 4],
                                     bank[6 + q][:, 0:4 * G].rearrange("p (j g) -> p g j", g=G), ACT.Copy)\
                    .then_inc(src_col_done, 1)
            for c in range(NCH):
                bs = chunk_blocks[c]
                act.wait_ge(q_ps, c + 1)
                nc.scalar.activation(q_out[:, bs.start:bs.stop, :],
                                     bank[4 + c % 2][:, 0:len(bs) * D].rearrange("p (b d) -> p b d", d=D), ACT.Copy)\
                    .then_inc(q_done, 1)

            def add_bu1(c):
                n0, n = chunk[c]
                act.wait_ge(xu_ps, c + 1)
                nc.scalar.activation(z[:, n0:n0 + n], bank[4 + c % 2][:, 0:n], ACT.Identity, bias=cols[:, 2:3])\
                    .then_inc(xu_done, 1)

            def squares(h, g2, k):
                s, at = (k // 2) % 2, (k % 2) * HALF
                act.wait_ge(dist_loaded[s], g2 * 16 + 16)
                nc.scalar.activation(feat[0:RADIAL, s, at:at + HALF], dist_b[0:RADIAL, s, at:at + HALF],
                                     ACT.Square, bias=offset[0:RADIAL, :]).then_inc(square_done, 1)

            def gaussians(h, k):
                s, at = (k // 2) % 2, (k % 2) * HALF
                act.wait_ge(square_done, h + 1)
                nc.scalar.activation(feat[0:RADIAL, s, at:at + HALF], feat[0:RADIAL, s, at:at + HALF],
                                     ACT.Exp, scale=-0.5 / (CUTOFF / (RADIAL - 1)) ** 2).then_inc(radial_ready, 1)

            def step(h, g2_next, k):
                if early(h):
                    act.wait_ge(xg_ps, h + 1)
                    if h >= 1:
                        act.wait_ge(pre_done, h)
                    nc.scalar.activation(xg[:, :], bank[6][:, :], ACT.Copy).then_inc(xg_ready, 1)
                if loops(h) or h < H:
                    n = half_edges(h)
                    act.wait_ge(pre_done, h + 1)
                    if later(h, 2):
                        act.wait_ge(h1_ready, h - 1)
                    nc.scalar.activation(th1[:, k % 2, 0:n], pre_ps[k % 2][:, 0:n], ACT.Tanh, scale=0.5)\
                        .then_inc(tanh1_done, 1)
                if loops(h) or h + 2 < H:
                    squares(h + 2, g2_next, (k + 2) % SLOTS)
                if loops(h) or 1 <= h <= H:
                    n = half_edges(h - 1)
                    act.wait_ge(l2_done, h)
                    if later(h, 3):
                        act.wait_ge(h2_ready, h - 2)
                    nc.scalar.activation(th2[:, (k - 1) % 2, 0:n], l2_ps[(k - 1) % 2][:, 0:n], ACT.Tanh, scale=0.5)\
                        .then_inc(tanh2_done, 1)
                if loops(h) or h + 2 < H:
                    gaussians(h + 2, (k + 2) % SLOTS)

            act.wait_ge(lane_done, 2)
            act.wait_ge(zeros_set, 2)
            for h in (0, 1):
                squares(h, 0, h)
                gaussians(h, h)
            act.wait_ge(weights_loaded, 16 * 16)
            for c in range(NCH):
                add_bu1(c)
            act.wait_ge(base_done, 1)
            with act.If(is_fast(act) > 0):
                for h in range(8):
                    step(h, (h + 2) // 4, h)
                with act.Fori(0, LOOPS) as i:
                    for k in range(SLOTS):
                        step(i * 8 + (8 + k), i * 2 + (2 + (k + 2) // 4), k)
                for h in range(H - 2, H + 1):
                    step(h, (h + 2) // 4, h % 8)
            with act.Else():
                with act.Fori(0, G) as g:
                    act.wait_ge(gen_dist_loaded, g * 16 + 16)
                    nc.scalar.activation(feat[0:RADIAL, 0, :], dist_b[0:RADIAL, 0, :], ACT.Square,
                                         bias=offset[0:RADIAL, :]).then_inc(gen_square_done, 1)
                    act.wait_ge(gen_square_done, g + 1)
                    nc.scalar.activation(feat[0:RADIAL, 0, :], feat[0:RADIAL, 0, :], ACT.Exp,
                                         scale=-0.5 / (CUTOFF / (RADIAL - 1)) ** 2).then_inc(gen_radial_ready, 1)
                    with act.Fori(0, NW) as w:
                        act.wait_ge(gen_pre_done, g * NW + w + 1)
                        for s in range(2):
                            a = nc.scalar.activation(th1[:, s, :], pre_ps[s][:, :], ACT.Tanh, scale=0.5)
                        a.then_inc(gen_tanh1_done, 1)
                        act.wait_ge(gen_l2_done, g * NW + w + 1)
                        for s in range(2):
                            a = nc.scalar.activation(th2[:, s, :], l2_ps[s][:, :], ACT.Tanh, scale=0.5)
                        a.then_inc(gen_tanh2_done, 1)

            act.wait_ge(edges_done, 1)
            for c in range(NCH + 1):
                if c < NCH:
                    n0, n = chunk[c]
                    nc.scalar.activation(s1[:, n0:n0 + n], z[:, n0:n0 + n], ACT.Silu).then_inc(s1_done, 1)
                if c >= 1:
                    n0, n = chunk[c - 1]
                    act.wait_ge(b_ps, c)
                    nc.scalar.activation(s2[:, n0:n0 + n], bank[(c - 1) % 2][:, 0:n], ACT.Silu, bias=bui[:, :])\
                        .then_inc(s2_done, 1)
            act.wait_ge(var_done, NCH)
            nc.scalar.activation(std[:, :], var[:, :], ACT.Sqrt, bias=eps[:, :], scale=1.0 / D).then_inc(std_done, 1)

        @block.vector
        def _(dve):
            chain = [0]

            def link(ins):
                chain[0] += 1
                ins.then_inc(v_chain, 1)
                dve.wait_ge(v_chain, chain[0])

            nc.vector.memset(dst_i[:, REST:GROUP], FAR).then_inc(pads_set, 1)
            nc.vector.memset(src_i[:, REST:GROUP], 0).then_inc(pads_set, 1)
            nc.vector.memset(left[32:WIN, :, :], 0.0).then_inc(zeros_set, 1)
            nc.vector.memset(xn[:, NB - 1, :], 0.0).then_inc(pads_set, 1)
            nc.vector.memset(feat[:, :, :], 1.0).then_inc(zeros_set, 1)
            nc.vector.memset(src_col[:, G:G + 3, :], 0)
            nc.vector.memset(eps[:, :], EPS)
            nc.vector.memset(var[:, :], 1.0)

            dve.wait_ge(dst_loaded, 32)
            link(nc.vector.tensor_copy(dst_f[0:G, :], dst_i[0:G, :]))
            nc.vector.tensor_reduce(least[0:G, 0:1], dst_f[0:G, 0:REST], AX.X, ALU.min)
            nc.vector.tensor_reduce(least[0:FULL, 1:2], dst_f[0:FULL, REST:GROUP], AX.X, ALU.min)
            nc.vector.tensor_reduce(most[0:G, 0:1], dst_f[0:G, 0:REST], AX.X, ALU.max)
            link(nc.vector.tensor_reduce(most[0:FULL, 1:2], dst_f[0:FULL, REST:GROUP], AX.X, ALU.max))
            nc.vector.tensor_tensor(least[0:FULL, 0:1], least[0:FULL, 0:1], least[0:FULL, 1:2], ALU.min)
            link(nc.vector.tensor_tensor(most[0:FULL, 0:1], most[0:FULL, 0:1], most[0:FULL, 1:2], ALU.max))
            link(nc.vector.tensor_scalar(base[0:G, 0:1], least[0:G, 0:1], float(N - WIN), None, ALU.min))
            link(nc.vector.tensor_tensor(wide[0:G, 1:2], most[0:G, 0:1], base[0:G, 0:1], ALU.subtract))
            nc.vector.tensor_scalar(wide[0:G, 0:1], wide[0:G, 1:2], -1.0 if force_general else float(WIN), None, ALU.is_ge)\
                .then_inc(wide_done, 1)
            def copy_p(c):
                bs = chunk_blocks[c]
                dve.wait_ge(p_ps, c + 1)
                nc.vector.tensor_copy(p_out[:, bs.start:bs.stop, :],
                                      bank[2 + c % 2][:, 0:len(bs) * D].rearrange("p (b d) -> p b d", d=D)).then_inc(p_done, 1)

            for c in range(2):
                copy_p(c)
            dve.wait_ge(wide_ps, 1)
            link(nc.vector.tensor_scalar(base[:, 2:3], bank[4][:, 0:1], 0.0, None, ALU.is_equal))
            nc.vector.tensor_copy(sorted_i[:, :], base[:, 2:3])
            link(nc.vector.tensor_tensor(base[0:G, 1:2], base[0:G, 0:1], base[0:G, 2:3], ALU.mult))
            nc.vector.tensor_copy(base_i[0:G, :], base[0:G, 1:2]).then_inc(base_done, 1)
            copy_p(2)
            nc.vector.tensor_scalar(dst_f[0:G, :], dst_f[0:G, :], base[0:G, 1:2], None, ALU.subtract).then_inc(rel_done, 1)
            for c in range(3, NCH):
                copy_p(c)
            dve.wait_ge(src_col_done, 2)
            nc.vector.tensor_scalar(index[:, 4:8, :].rearrange("p s t -> p (s t)"),
                                    src_col[:, 2:4, :].rearrange("p g t -> p (g t)"), 0.0, None, ALU.add)\
                .then_inc(index_ready, 8)
            dve.wait_ge(pool_const, 6)
            dve.wait_ge(lane_done, 1)
            nc.vector.tensor_scalar(offset[:, :], lane[:, :], float(WIN), -CUTOFF / (RADIAL - 1), ALU.add, ALU.mult)\
                .then_inc(lane_done, 1)
            nc.vector.tensor_copy(win[:, :], win_i[:, :])
            dve.wait_ge(b2_loaded, 16)
            link(nc.vector.tensor_copy(b2_part[:, 0, :], b2_row[:, :]))
            link(nc.vector.tensor_tensor(b2_left[:, 0, :], b2_row[:, :], b2_part[:, 0, :], ALU.subtract))
            link(nc.vector.tensor_copy(b2_part[:, 1, :], b2_left[:, 0, :]))
            link(nc.vector.tensor_tensor(b2_left[:, 1, :], b2_left[:, 0, :], b2_part[:, 1, :], ALU.subtract))
            nc.vector.tensor_copy(b2_part[:, 2, :], b2_left[:, 1, :]).then_inc(b2_loaded, 1)
            dve.wait_ge(tables_ps, 1)
            for q in range(2):
                nc.vector.tensor_copy(rel_col[:, 0:G, 4 * q:4 * q + 4],
                                      bank[6 + q][:, 0:4 * G].rearrange("p (j g) -> p g j", g=G)).then_inc(tables_done, 1)
            dve.wait_ge(weights_loaded, 16 * 16)
            nc.vector.tensor_scalar(w2half[:, :], w2[:, :], 0.5, None, ALU.mult)
            dve.wait_ge(tables_done, 2)

            def take_turned():
                dve.wait_ge(turn_ps, 1)
                nc.vector.tensor_scalar(w3t[:, :], bank[7][:, 0:D], 0.5, None, ALU.mult).then_inc(turned, 1)
                nc.vector.tensor_copy(wu2t[:, :], bank[7][:, D:2 * D]).then_inc(turned, 1)

            def take_folded():
                dve.wait_ge(fold_ps, 1)
                nc.vector.tensor_copy(w3u[:, :], bank[7][:, 0:D])
                nc.vector.tensor_copy(wui[:, :], bank[7][:, D:2 * D])
                nc.vector.tensor_copy(b3u[:, :], bank[7][:, 2 * D:2 * D + 1])
                nc.vector.tensor_tensor(bui[:, :], bank[7][:, 2 * D + 1:2 * D + 2], cols[:, 3:4], ALU.add).then_inc(folded, 1)

            def center_wi2():
                link(nc.vector.tensor_reduce(wi2_mean[:, :], wi2[:, :], AX.X, ALU.add))
                link(nc.vector.tensor_scalar(wi2_mean[:, :], wi2_mean[:, :], 1.0 / D, None, ALU.mult))
                nc.vector.tensor_scalar(wi2c[:, :], wi2[:, :], wi2_mean[:, 0:1], None, ALU.subtract).then_inc(wi2_done, 1)

            def center_x(b0, b1):
                xb = xn[:, b0:b1, :]
                link(nc.vector.tensor_tensor(xb, xb, bi2_all[:, :].rearrange("p (a d) -> p a d", a=1)
                                             .broadcast_to([P, b1 - b0, D]), ALU.add))
                link(nc.vector.tensor_reduce(xb_mean[:, b0:b1], xb, AX.X, ALU.add))
                link(nc.vector.tensor_scalar(xb_mean[:, b0:b1], xb_mean[:, b0:b1], 1.0 / D, None, ALU.mult))
                nc.vector.tensor_tensor(xb, xb, xb_mean[:, b0:b1].rearrange("p (b a) -> p b a", a=1)
                                        .broadcast_to([P, b1 - b0, D]), ALU.subtract).then_inc(xb_done, 1)

            def take_index(h, g, k):
                nc.vector.tensor_scalar(index[:, k, :], src_col[:, bass.ds(g, 1), (k % 2) * HT:(k % 2 + 1) * HT]
                                        .rearrange("p a t -> p (a t)"), 0.0, None, ALU.add).then_inc(index_ready, 1)

            def one_hot(h, g2, k):
                s, at = (k // 2) % 2, (k % 2) * HALF
                dve.wait_ge(rel_loaded[s], g2 * 16 + 16)
                nc.vector.tensor_scalar(feat[WIN:P, s, at:at + HALF], rel_b[WIN:P, s, at:at + HALF],
                                        lane[WIN:P, :], None, ALU.is_equal).then_inc(one_hot_ready, 1)

            def hot_edges(g, s):
                nc.vector.tensor_tensor(hot[:, s, :, :],
                                        win[:, :].rearrange("p (a w) -> p a w", a=1).broadcast_to([P, GT, WIN]),
                                        rel_col[:, bass.ds(g, 1), :].rearrange("p a t -> p (a t)")
                                        .rearrange("p (t a) -> p t a", a=1).broadcast_to([P, GT, WIN]),
                                        ALU.is_equal).then_inc(hot_ready, 1)

            def take_sums(g, s):
                b = dve.value_load(base_sb[0:1, bass.ds(g, 1)], min_val=0, max_val=N - WIN)
                if later(g, 1):
                    dve.wait_ge(z_added, g * 2 - 1)
                nc.vector.tensor_copy(win_sum[:, s, :], agg_ps[s][:, 0:WIN]).then_inc(win_ready, 1)
                at = z[:, bass.ds(b, WIN)]
                nc.vector.scalar_tensor_tensor(out=at, in0=agg_ps[s][:, WIN:2 * WIN], scalar=b3u[:, :], in1=at,
                                               op0=ALU.mult, op1=ALU.add).then_inc(z_added, 1)

            def add_window(g, s):
                b = dve.value_load(base_sb[0:1, bass.ds(g, 1)], min_val=0, max_val=N - WIN)
                dve.wait_ge(win_ps, g + 1)
                dve.wait_ge(z_added, g * 2 + (1 if not loops(g) and g == G - 1 else 2))
                at = z[:, bass.ds(b, WIN)]
                nc.vector.tensor_tensor(at, at, bank[6 + s][:, 0:WIN], ALU.add).then_inc(z_added, 1)

            def step(h, g, g2_next, k):
                s = (k // 2) % 2
                if loops(h) or h < H:
                    n = half_edges(h)
                    dve.wait_ge(tanh1_done, h + 1)
                    if later(h, 2):
                        dve.wait_ge(l2_done, h - 1)
                    nc.vector.scalar_tensor_tensor(out=h1[:, k % 2, 0:n], in0=th1[:, k % 2, 0:n], scalar=1.0,
                                                   in1=pre_ps[k % 2][:, 0:n], op0=ALU.add, op1=ALU.mult).then_inc(h1_ready, 1)
                if loops(h) or h + 8 < H:
                    take_index(h + 8, g + 4, k)
                if loops(h) or h + 2 < H:
                    one_hot(h + 2, g2_next, (k + 2) % SLOTS)
                if k % 2 == 0:
                    if later(g, 2):
                        dve.wait_ge(seg_done, h - 2)
                        take_sums(g - 2, s)
                    if loops(g) or g < G:
                        hot_edges(g, s)
                if loops(h) or 1 <= h <= H:
                    n = half_edges(h - 1)
                    dve.wait_ge(tanh2_done, h)
                    if later(h, 3):
                        dve.wait_ge(seg_done, h - 2)
                    nc.vector.scalar_tensor_tensor(out=h2[:, (k - 1) % 2, 0:n], in0=th2[:, (k - 1) % 2, 0:n], scalar=1.0,
                                                   in1=l2_ps[(k - 1) % 2][:, 0:n], op0=ALU.add, op1=ALU.mult)\
                        .then_inc(h2_ready, 1)
                if k % 2 == 0 and later(g, 3):
                    add_window(g - 3, 1 - s)

            take_turned()
            take_folded()
            center_wi2()
            with dve.If(is_fast(dve) > 0):
                for h in (0, 1):
                    one_hot(h, 0, h)
                for h in range(8):
                    if h == 4:
                        dve.wait_ge(base_loaded, 16)
                        dve.wait_ge(xu_done, NCH)
                    step(h, h // 2, (h + 2) // 4, h)
                    if h >= 4:
                        center_x(NB * (h - 4) // 4, NB * (h - 3) // 4)
                with dve.Fori(0, LOOPS) as i:
                    for k in range(SLOTS):
                        step(i * 8 + (8 + k), i * 4 + (4 + k // 2), i * 2 + (2 + (k + 2) // 4), k)
                for h in range(H - 2, H + 1):
                    step(h, h // 2, (h + 2) // 4, h % 8)
                dve.wait_ge(seg_done, H)
                take_sums(G - 1, (G - 1) % 2)
                add_window(G - 2, G % 2)
                add_window(G - 1, (G - 1) % 2)
                dve.wait_ge(z_added, 2 * G)
            with dve.Else():
                center_x(0, NB)
                dve.wait_ge(xu_done, NCH)
                dve.wait_ge(gathered[0], 16 * HT)
                dve.wait_ge(gathered[1], 16 * HT)
                nc.vector.memset(wide[:, :], 0.0).then_inc(gen_added, 1)
                with dve.Fori(0, G) as g:
                    dve.wait_ge(gen_added, g * NW + 1)
                    nc.vector.tensor_scalar(index[:, 0:2, :].rearrange("p s t -> p (s t)"),
                                            src_col[:, bass.ds(g, 1), :].rearrange("p a t -> p (a t)"), 0.0, None,
                                            ALU.add).then_inc(gen_index_ready, 1)
                    nc.vector.tensor_scalar(rel_col[:, G, :], rel_col[:, bass.ds(g, 1), :].rearrange("p a t -> p (a t)"),
                                            0.0, None, ALU.add).then_inc(gen_rel_ready, 1)
                    with dve.Fori(0, NW) as w:
                        dve.wait_ge(gen_rel_loaded, g * 16 + 16)
                        dve.wait_ge(gen_rel_ready, g * (NW + 1) + w + 1)
                        nc.vector.tensor_scalar(feat[WIN:P, 0, :], rel_b[WIN:P, 0, :], lane[WIN:P, :], None, ALU.is_equal)
                        nc.vector.tensor_tensor(hot[:, 0, :, :],
                                                win[:, :].rearrange("p (a w) -> p a w", a=1).broadcast_to([P, GT, WIN]),
                                                rel_col[:, G, :].rearrange("p (t a) -> p t a", a=1)
                                                .broadcast_to([P, GT, WIN]), ALU.is_equal).then_inc(gen_hot_ready, 1)
                        dve.wait_ge(gen_hot_ready, g * NW + w + 1)
                        nc.vector.tensor_scalar(rel_b[WIN:P, 0, :], rel_b[WIN:P, 0, :], float(WIN), None, ALU.subtract)
                        nc.vector.tensor_scalar(rel_col[:, G, :], rel_col[:, G, :], float(WIN), None, ALU.subtract)\
                            .then_inc(gen_rel_ready, 1)
                        dve.wait_ge(gen_tanh1_done, g * NW + w + 1)
                        for s in range(2):
                            m = nc.vector.scalar_tensor_tensor(out=h1[:, s, :], in0=th1[:, s, :], scalar=1.0,
                                                               in1=pre_ps[s][:, :], op0=ALU.add, op1=ALU.mult)
                        m.then_inc(gen_h1_ready, 1)
                        dve.wait_ge(gen_tanh2_done, g * NW + w + 1)
                        for s in range(2):
                            m = nc.vector.scalar_tensor_tensor(out=h2[:, s, :], in0=th2[:, s, :], scalar=1.0,
                                                               in1=l2_ps[s][:, :], op0=ALU.add, op1=ALU.mult)
                        m.then_inc(gen_h2_ready, 1)
                        dve.wait_ge(gen_seg_done, g * NW + w + 1)
                        nc.vector.tensor_copy(win_sum[:, 0, :], agg_ps[0][:, 0:WIN]).then_inc(gen_win_ready, 1)
                        at = z[:, bass.ds(w * WIN, WIN)]
                        nc.vector.scalar_tensor_tensor(out=at, in0=agg_ps[0][:, WIN:2 * WIN], scalar=b3u[:, :], in1=at,
                                                       op0=ALU.mult, op1=ALU.add).then_inc(z_added, 1)
                        dve.wait_ge(gen_win_ps, g * NW + w + 1)
                        dve.wait_ge(z_added, g * NW + w + 1)
                        nc.vector.tensor_tensor(at, at, bank[6][:, 0:WIN], ALU.add).then_inc(gen_added, 1)
                dve.wait_ge(gen_added, G * NW + 1)
            nc.vector.memset(wide[:, :], 0.0).then_inc(edges_done, 1)

            def sum_squares(c):
                bs = chunk_blocks[c]
                m = min(P, NCOL - bs.start * P)
                dve.wait_ge(y2_done, c + 1)
                nc.vector.tensor_reduce(var[0:m, bs.start:bs.stop],
                                        y2[0:m, c % 2, 0:len(bs) * D].rearrange("p (b d) -> p b d", d=D), AX.X, ALU.add)\
                    .then_inc(var_done, 1)

            for c in range(NCH):
                bs = chunk_blocks[c]
                m = min(P, NCOL - bs.start * P)
                nb, yc = len(bs), y[:, bs.start:bs.stop, :]
                dve.wait_ge(c_ps, c + 1)
                nc.vector.tensor_tensor(yc[0:m], xn[0:m, bs.start:bs.stop, :],
                                        bank[2 + c % 2][0:m, 0:nb * D].rearrange("p (b d) -> p b d", d=D), ALU.add)\
                    .then_inc(y_done, 1)
                if c >= 1:
                    sum_squares(c - 1)
            sum_squares(NCH - 1)
            dve.wait_ge(std_done, 1)
            nc.vector.reciprocal(rstd[:, :], std[:, :]).then_inc(rstd_done, 1)
            dve.wait_ge(rstd_done, 1)
            for c in range(NCH):
                bs = chunk_blocks[c]
                m = min(P, NCOL - bs.start * P)
                nc.vector.tensor_tensor(res[0:m, bs.start:bs.stop, :], y[0:m, bs.start:bs.stop, :],
                                        rstd[0:m, bs.start:bs.stop].rearrange("p (b a) -> p b a", a=1)
                                        .broadcast_to([m, len(bs), D]), ALU.mult).then_inc(res_done, 1)


_INS = ['x', 'src', 'dst', 'edge_weight', 'L0_gnn_Wm1', 'L0_gnn_bm1', 'L0_gnn_Wm2', 'L0_gnn_bm2', 'L0_gnn_Wm3',
        'L0_gnn_bm3', 'L0_gnn_Wu1', 'L0_gnn_bu1', 'L0_gnn_Wu2', 'L0_gnn_bu2', 'L0_gnn_Wi1', 'L0_gnn_bi1',
        'L0_gnn_Wi2', 'L0_gnn_bi2']
_OUT = ((3125, 128), 'float32')


def kernel(**inputs):
    import numpy as _np
    import concourse.bacc as _bacc
    from concourse import mybir as _mybir
    from concourse.bass_utils import run_bass_kernel_spmd as _run

    nc = _bacc.Bacc("TRN2", target_bir_lowering=False, num_devices=1)
    arrays, args = {}, []
    for name in _INS:
        a = _np.ascontiguousarray(inputs[name])
        arrays[f"in_{name}_dram"] = a
        args.append(nc.dram_tensor(f"in_{name}_dram", a.shape, _mybir.dt.from_np(a.dtype), kind="ExternalInput").ap())
    out = nc.dram_tensor("out_0_dram", _OUT[0], _mybir.dt.from_np(_np.dtype(_OUT[1])), kind="ExternalOutput").ap()
    gnn_kernel(nc, *args, out)
    r = _run(nc, [arrays], core_ids=[0])
    return r.results[0]["out_0_dram"]
```

```python
from contextlib import ExitStack

import concourse.bass as bass
from concourse import mybir

F32 = mybir.dt.float32
BF16 = mybir.dt.bfloat16
I32 = mybir.dt.int32
ALU = mybir.AluOpType
ACT = mybir.ActivationFunctionType
AX = mybir.AxisListType

P = 128
RADIAL = 50
CUTOFF = 10.0
EPS = 1e-5
WIN = 64
TILE = 128
HALF = 512
HT = HALF // TILE
GROUP = 2 * HALF
GT = GROUP // TILE
SLOTS = 8
HOT_HALF = 1
HOT_PARTS = 5
FAR = 8191


def gnn_kernel(nc, x, src, dst, dist, Wm1, bm1, Wm2, bm2, Wm3, bm3, Wu1, bu1, Wu2, bu2, Wi1, bi1,
               Wi2, bi2, out, force_general=False, force_redo=False):
    N, D = x.shape
    E = src.shape[0]
    assert D == P
    NB = -(-N // P)
    NPAD = NB * P
    NW = -(-N // WIN)
    NCOL = NW * WIN
    G = -(-E // GROUP)
    H = 2 * G
    FULL = E // GROUP
    REST = E - FULL * GROUP
    assert G == FULL + 1 and G % 4 == 1 and G >= 9 and G <= P
    LOOPS = (H - 10) // SLOTS
    LASTN = N - (NB - 1) * P
    NCH = -(-NCOL // HALF)
    chunk = [(HALF * c, min(HALF, NCOL - HALF * c)) for c in range(NCH)]
    chunk_blocks = [range(4 * c, min(4 * c + 4, NB)) for c in range(NCH)]
    EARLY = NCH - 2
    late_pieces = [(b * P, min(2 * P, NCOL - b * P), range(b, min(b + 2, NB))) for b in range(4 * EARLY, NB, 2)]
    FIRST_EARLY = H - 2 - EARLY * SLOTS
    pending = [(FIRST_EARLY + n * SLOTS) // 2 - 2 for n in range(EARLY)]

    with ExitStack() as ctx:
        def sb(name, shape, dt=F32):
            return ctx.enter_context(nc.sbuf_tensor(name, shape, dt))

        def sem(name):
            return ctx.enter_context(nc.semaphore(name))

        p_rows = nc.dram_tensor("p_rows", (NPAD, D), F32).ap()
        q_rows = nc.dram_tensor("q_rows", (NPAD, D), F32).ap()
        rel_rows = nc.dram_tensor("rel_rows", (G, GROUP), F32).ap()
        src_rows = nc.dram_tensor("src_rows", (G, GROUP), F32).ap()
        base_row = nc.dram_tensor("base_row", (1, G), I32).ap()

        bank = [ctx.enter_context(nc.psum_tensor(f"bank{n}", [P, HALF], F32)) for n in range(8)]
        pre_ps, l2_ps, agg_ps = bank[0:2], bank[2:4], bank[4:6]

        w1a = sb("w1a", [P, D])
        w1b = sb("w1b", [P, D])
        w2 = sb("w2", [P, D])
        w2half = sb("w2half", [P, D])
        w3 = sb("w3", [P, D])
        w3t = sb("w3t", [P, D])
        wu1a = sb("wu1a", [P, D])
        wu1b = sb("wu1b", [P, D])
        wu2 = sb("wu2", [P, D])
        wu2t = sb("wu2t", [P, D])
        wi1 = sb("wi1", [P, D])
        wi2 = sb("wi2", [P, D])
        w3u = sb("w3u", [P, D])
        wui = sb("wui", [P, D])
        bi2_all = sb("bi2_all", [P, D])
        wi2c = sb("wi2c", [P, D])
        wi2_mean = sb("wi2_mean", [P, 1])
        cols = sb("cols", [P, 4])
        b3u = sb("b3u", [P, 1])
        bui = sb("bui", [P, 1])
        bui_half = sb("bui_half", [P, 1])
        b2_row = sb("b2_row", [1, D])
        b2_part = sb("b2_part", [1, 3, D], BF16)
        b2_left = sb("b2_left", [1, 2, D])
        b2_rhs = sb("b2_rhs", [3, HT, D], BF16)
        ones_bf = sb("ones_bf", [P, P], BF16)
        ones_f = sb("ones_f", [P, P])
        ident = sb("ident", [P, P])
        lane = sb("lane", [P, 1])
        lane_i = sb("lane_i", [P, 1], I32)
        offset = sb("offset", [P, 1])
        rate = sb("rate", [P, 1])
        win_i = sb("win_i", [P, WIN], I32)
        win = sb("win", [P, WIN])
        eps = sb("eps", [P, 1])

        xn = sb("xn", [P, NB, D])
        xt = sb("xt", [P, NPAD])
        y = xt[:, :].rearrange("p (b d) -> p b d", d=D)
        p_out = sb("p_out", [P, NB, D])
        q_out = sb("q_out", [P, NB, D])
        s1 = p_out[:, :, :].rearrange("p b d -> p (b d)")
        s2 = q_out[:, :, :].rearrange("p b d -> p (b d)")
        z = sb("z", [P, NPAD])
        xb_mean = sb("xb_mean", [P, NB])
        xg = sb("xg", [P, 4, HALF])
        win_sum = sb("win_sum", [P, 2, WIN])

        src_i = sb("src_i", [P, GROUP], I32)
        dst_i = sb("dst_i", [P, GROUP], I32)
        src_f = sb("src_f", [P, GROUP])
        dst_f = sb("dst_f", [P, GROUP])
        least = sb("least", [P, 2])
        most = sb("most", [P, 2])
        base = sb("base", [P, 3])
        base_i = sb("base_i", [P, 1], I32)
        wide = sb("wide", [P, 2])
        sorted_i = sb("sorted_i", [P, 1], I32)
        base_sb = sb("base_sb", [1, G], I32)
        src_col = sb("src_col", [P, G + 3, GT], I32)
        rel_col = sb("rel_col", [P, G + 1, GT])

        index = sb("index", [P, SLOTS, HT], I32)
        rows = sb("rows", [P, SLOTS, HT, D])
        near = sb("near", [P, 2, GROUP])
        feat = sb("feat", [P, 2, GROUP])
        left = sb("left", [P, 2, D])
        hot = sb("hot", [P, 2, GT, WIN])
        hot_count = sb("hot_count", [P, 2, WIN])
        node_i = sb("node_i", [P, NB], I32)
        node = sb("node", [P, NB])
        src_b = sb("src_b", [P, TILE])
        src_hot = sb("src_hot", [P, NB, TILE])
        th1 = sb("th1", [P, 2, HALF])
        h1 = sb("h1", [P, 2, HALF])
        th2 = sb("th2", [P, 2, HALF])
        h2 = sb("h2", [P, 2, HALF])
        tu = sb("tu", [P, 2, HALF])
        s1_early = sb("s1_early", [P, HALF])
        s2_early = sb("s2_early", [P, HALF])
        y2 = sb("y2", [P, 2, HALF])
        base_f = sb("base_f", [1, G])
        lowest = sb("lowest", [1, 3, EARLY])
        redo_i = sb("redo_i", [1, 1], I32)
        var = sb("var", [P, NB])
        std = sb("std", [P, NB])
        rstd = sb("rstd", [P, NB])
        res = p_out

        x_loaded = [sem(f"x_loaded{n}") for n in range(3)]
        first_index = sem("first_index")
        weights_loaded = sem("weights_loaded")
        edges_loaded = sem("edges_loaded")
        dst_loaded = sem("dst_loaded")
        b2_loaded = sem("b2_loaded")
        b2_placed = sem("b2_placed")
        pool_const = sem("pool_const")
        pads_set = sem("pads_set")
        zeros_set = sem("zeros_set")
        v_chain = sem("v_chain")
        src_done = sem("src_done")
        src_ps = sem("src_ps")
        src_col_done = sem("src_col_done")
        xt_ps_done = sem("xt_ps_done")
        xt_done = sem("xt_done")
        p_ps = sem("p_ps")
        p_done = sem("p_done")
        q_ps = sem("q_ps")
        q_done = sem("q_done")
        w1a_loaded = sem("w1a_loaded")
        w1b_loaded = sem("w1b_loaded")
        p_stored = sem("p_stored")
        q_stored = sem("q_stored")
        tables_ps = sem("tables_ps")
        tables_done = sem("tables_done")
        wide_done = sem("wide_done")
        wide_ps = sem("wide_ps")
        base_done = sem("base_done")
        rel_done = sem("rel_done")
        rel_stored = sem("rel_stored")
        base_stored = sem("base_stored")
        base_loaded = sem("base_loaded")
        turn_ps = sem("turn_ps")
        turned = sem("turned")
        fold_ps = sem("fold_ps")
        folded = sem("folded")
        xu_ps = sem("xu_ps")
        xu_done = sem("xu_done")
        lane_done = sem("lane_done")
        index_ready = sem("index_ready")
        index_seen = sem("index_seen")
        gathered = [sem(f"gathered{n}") for n in range(SLOTS)]
        dist_loaded = [sem(f"dist_loaded{n}") for n in range(2)]
        rel_loaded = [sem(f"rel_loaded{n}") for n in range(2)]
        q_loaded = [sem(f"q_loaded{n}") for n in range(2)]
        square_done = sem("square_done")
        radial_ready = sem("radial_ready")
        pre_done = sem("pre_done")
        tanh1_done = sem("tanh1_done")
        h1_ready = sem("h1_ready")
        l2_done = sem("l2_done")
        tanh2_done = sem("tanh2_done")
        h2_ready = sem("h2_ready")
        hot_ready = sem("hot_ready")
        count_ready = sem("count_ready")
        src_stored = sem("src_stored")
        src_b_loaded = sem("src_b_loaded")
        src_hot_ready = sem("src_hot_ready")
        seg_done = sem("seg_done")
        xg_ps = sem("xg_ps")
        xg_ready = sem("xg_ready")
        win_ready = sem("win_ready")
        win_ps = sem("win_ps")
        z_added = sem("z_added")
        gen_added = sem("gen_added")
        gen_index_ready = sem("gen_index_ready")
        gen_gathered = sem("gen_gathered")
        gen_dist_loaded = sem("gen_dist_loaded")
        gen_square_done = sem("gen_square_done")
        gen_radial_ready = sem("gen_radial_ready")
        gen_rel_loaded = sem("gen_rel_loaded")
        gen_rel_ready = sem("gen_rel_ready")
        gen_q_loaded = sem("gen_q_loaded")
        gen_hot_ready = sem("gen_hot_ready")
        gen_count_ready = sem("gen_count_ready")
        gen_pre_done = sem("gen_pre_done")
        gen_tanh1_done = sem("gen_tanh1_done")
        gen_h1_ready = sem("gen_h1_ready")
        gen_l2_done = sem("gen_l2_done")
        gen_tanh2_done = sem("gen_tanh2_done")
        gen_h2_ready = sem("gen_h2_ready")
        gen_seg_done = sem("gen_seg_done")
        gen_win_ready = sem("gen_win_ready")
        gen_win_ps = sem("gen_win_ps")
        edges_done = sem("edges_done")
        redo_set = sem("redo_set")
        early_out = sem("early_out")
        late_out = sem("late_out")

        def update_sems(name):
            return {what: sem(f"{name}_{what}") for what in
                    ("t1_done", "s1_done", "b_ps", "t2_done", "s2_done", "c_ps", "y_done", "y2_done", "var_done",
                     "std_done", "rstd_done", "res_done")}

        early_up, late_up, redo_up = (update_sems(name) for name in ("early", "late", "redo"))
        pieces = [(*chunk[c], chunk_blocks[c]) for c in range(NCH)]
        early_run = (pieces[0:EARLY], early_up, bank[7:8], bank[7:8])
        late_run = (late_pieces, late_up, bank[0:2], bank[2:4])
        redo_run = (pieces, redo_up, bank[0:2], bank[2:4])
        x_flat, y_flat = xn[:, :, :].rearrange("p b d -> p (b d)"), xt

        class Place:
            def __init__(self, run, n):
                parts, _, b_banks, c_banks = run
                self.b_bank, self.c_bank = (banks[n % len(banks) if not loops(n) else 0] for banks in (b_banks, c_banks))
                if loops(n):
                    self.size, self.nodes, self.count = HALF, P, HALF // P
                    self.cols = self.rows = bass.ds(n * HALF, HALF)
                    self.blocks = bass.ds(n * (HALF // P), HALF // P)
                    self.s1, self.s2, self.slot = s1_early[:, :], s2_early[:, :], 0
                else:
                    n0, self.size, bs = parts[n]
                    self.nodes, self.count = min(P, NCOL - bs.start * P), len(bs)
                    self.cols, self.rows = slice(n0, n0 + self.size), slice(bs.start * P, bs.stop * P)
                    self.blocks = slice(bs.start, bs.stop)
                    self.s1, self.s2, self.slot = s1[:, self.cols], s2[:, self.cols], n % 2
        xb_done = sem("xb_done")
        wi2_done = sem("wi2_done")

        block = ctx.enter_context(nc.Block())
        LASTT = -(-(REST - HALF) // TILE) if REST > HALF else 1
        XA, XB = 4, 12
        dst_whole = dst[0:FULL * GROUP].rearrange("(g e) -> g e", e=GROUP)
        src_whole = src[0:FULL * GROUP].rearrange("(g e) -> g e", e=GROUP)
        dst_rest = dst[FULL * GROUP:E].rearrange("(a e) -> a e", a=1)
        src_rest = src[FULL * GROUP:E].rearrange("(a e) -> a e", a=1)
        dist_row = dist.rearrange("(a e) -> a e", a=1)

        def loops(h):
            return not isinstance(h, int)

        def later(h, first):
            return loops(h) or h >= first

        def early(h):
            return not loops(h) and h < 4

        def half_edges(h):
            return LASTT * TILE if not loops(h) and h == H - 1 else HALF

        def hot_tile(h, k, n):
            return loops(h) and k == HOT_HALF and n is None

        def row_of(v):
            return v.rearrange("(a d) -> a d", a=1)

        def col_of(v):
            return v.rearrange("(d a) -> d a", a=1)

        def is_fast(eng):
            return eng.value_load(sorted_i[0:1, 0:1], min_val=0, max_val=1)

        def divide(eng, piece):
            bs = piece[2]
            m = min(P, NCOL - bs.start * P)
            return eng.tensor_tensor(res[0:m, bs.start:bs.stop, :], y[0:m, bs.start:bs.stop, :],
                                     rstd[0:m, bs.start:bs.stop].rearrange("p (b a) -> p b a", a=1)
                                     .broadcast_to([m, len(bs), D]), ALU.mult)

        def is_redo(eng):
            return eng.value_load(redo_i[0:1, 0:1], min_val=0, max_val=1)

        def blocks_of(run):
            return slice(run[0][0][2].start, run[0][-1][2].stop)

        @block.sync
        def _(sp):
            sp.dma_start(index[:, 0:4, :].rearrange("p s t -> p (s t)"),
                         src[0:4 * HALF].rearrange("(c p) -> p c", p=P), allow_slow_non_contiguous=True).then_inc(first_index, 16)
            sp.dma_start(xn[:, 0:XA, :], x[0:XA * P, :].rearrange("(b p) d -> p b d", p=P)).then_inc(x_loaded[0], 16)
            sp.dma_start(w1a[:, :], Wm1[0:D, :]).then_inc(w1a_loaded, 16)
            sp.dma_start(xn[:, XA:XB, :], x[XA * P:XB * P, :].rearrange("(b p) d -> p b d", p=P)).then_inc(x_loaded[1], 16)
            sp.dma_start(xn[:, XB:NB - 1, :],
                         x[XB * P:(NB - 1) * P, :].rearrange("(b p) d -> p b d", p=P)).then_inc(x_loaded[2], 16)
            sp.wait_ge(pads_set, 3)
            sp.dma_start(src_i[0:FULL, :], src_whole).then_inc(edges_loaded, 16)
            sp.dma_start(src_i[FULL:G, 0:REST], src_rest).then_inc(edges_loaded, 16)
            sp.dma_start(xn[0:LASTN, NB - 1, :], x[(NB - 1) * P:N, :]).then_inc(x_loaded[2], 16)
            sp.dma_start(w1b[:, :], Wm1[D:2 * D, :]).then_inc(w1b_loaded, 16)
            sp.dma_start(b2_row[:, :], row_of(bm2)).then_inc(b2_loaded, 16)
            sp.wait_ge(zeros_set, 1)
            sp.dma_start(left[0:RADIAL, 0, :], Wm1[2 * D:2 * D + RADIAL, :]).then_inc(weights_loaded, 16)
            sp.dma_start(left[0:RADIAL, 1, :], Wm1[2 * D:2 * D + RADIAL, :]).then_inc(weights_loaded, 16)
            for s in range(2):
                sp.dma_start(left[RADIAL:RADIAL + 1, s, :], row_of(bm1)).then_inc(weights_loaded, 16)
            for tile_, dram in ((w2, Wm2), (w3, Wm3), (wu1a, Wu1[0:D, :]), (wu1b, Wu1[D:2 * D, :]),
                                (wu2, Wu2), (wi1, Wi1), (wi2, Wi2),
                                (bi2_all, row_of(bi2).broadcast_to([P, D]))):
                sp.dma_start(tile_[:, :], dram).then_inc(weights_loaded, 16)
            for n, v in enumerate((bm3, bu2, bu1, bi1)):
                sp.dma_start(cols[:, n:n + 1], col_of(v)).then_inc(weights_loaded, 16)

            def load_dist(g, s, edges=GROUP):
                sp.dma_start(near[0:RADIAL, s, 0:edges],
                             dist_row[:, bass.ds(g * GROUP, edges)].broadcast_to([RADIAL, edges])).then_inc(dist_loaded[s], 16)

            def load_rel(g, s):
                sp.dma_start(near[WIN:P, s, :],
                             rel_rows[bass.ds(g, 1), :].broadcast_to([WIN, GROUP])).then_inc(rel_loaded[s], 16)

            def store_rows(c, done, made, rows_out, stored):
                bs = slice(chunk_blocks[c].start, chunk_blocks[c].stop)
                sp.wait_ge(done, c + 1)
                sp.dma_start(rows_out[bs.start * P:bs.stop * P, :].rearrange("(b p) d -> p b d", p=P), made[:, bs, :])\
                    .then_inc(stored, 16)

            for c in range(NCH):
                store_rows(c, p_done, p_out, p_rows, p_stored)
                if c == 1:
                    sp.wait_ge(base_done, 1)
                    sp.dma_start(base_row.rearrange("a g -> g a"), base_i[0:G, :]).then_inc(base_stored, 16)
                    sp.wait_ge(rel_done, 1)
                    sp.dma_start(rel_rows, dst_f[0:G, :]).then_inc(rel_stored, 16)
                if c == 3:
                    sp.wait_ge(base_stored, 16)
                    sp.dma_start(base_sb[:, :], base_row).then_inc(base_loaded, 16)
            sp.wait_ge(zeros_set, 2)
            for g in range(2):
                load_dist(g, g)
            sp.wait_ge(rel_stored, 16)
            for g in range(2):
                load_rel(g, g)
            sp.wait_ge(b2_loaded, 17)
            for n in range(3):
                sp.dma_start(b2_rhs[n:n + 1, :, :],
                             b2_part[:, n:n + 1, :].broadcast_to([1, HT, D])).then_inc(b2_placed, 16)
            for c in range(NCH):
                store_rows(c, q_done, q_out, q_rows, q_stored)
            sp.wait_ge(src_done, 1)
            sp.dma_start(src_rows, src_f[0:G, :]).then_inc(src_stored, 16)
            sp.wait_ge(base_loaded, 16)

            def load_q(b, s):
                sp.dma_start(left[WIN:P, s, :], q_rows[bass.ds(b, WIN), :]).then_inc(q_loaded[s], 16)

            def group_base(g):
                return sp.value_load(base_sb[0:1, bass.ds(g, 1)], min_val=0, max_val=N - WIN)

            def load_group(g, s, g_before, edges=GROUP):
                b = group_base(g)
                sp.wait_ge(square_done, g_before)
                load_dist(g, s, edges)
                load_rel(g, s)
                sp.wait_ge(pre_done, g_before)
                load_q(b, s)

            def general_loads(g, edges):
                sp.wait_ge(gen_added, g * NW + 1)
                sp.dma_start(near[0:RADIAL, 0, 0:edges], dist_row[:, bass.ds(g * GROUP, edges)].broadcast_to([RADIAL, edges]))\
                    .then_inc(gen_dist_loaded, 16)
                sp.dma_start(near[WIN:P, 0, :], rel_rows[bass.ds(g, 1), :].broadcast_to([WIN, GROUP]))\
                    .then_inc(gen_rel_loaded, 16)
                with sp.Fori(0, NW) as w:
                    sp.wait_ge(gen_added, w + (g * NW + 1))
                    sp.dma_start(left[WIN:P, 0, :], q_rows[bass.ds(w * WIN, WIN), :]).then_inc(gen_q_loaded, 16)

            def store_out(run, stored):
                parts, up, _, _ = run
                stores = 0
                for n, (_, _, bs) in enumerate(parts):
                    sp.wait_ge(up["res_done"], n + 1)
                    whole = min(bs.stop, NB - 1)
                    if whole > bs.start:
                        sp.dma_start(out[bs.start * P:whole * P, :].rearrange("(b p) d -> p b d", p=P),
                                     res[:, bs.start:whole, :]).then_inc(stored, 16)
                        stores += 1
                    if bs.stop == NB:
                        sp.dma_start(out[(NB - 1) * P:N, :], res[0:LASTN, NB - 1, :]).then_inc(stored, 16)
                        stores += 1
                return stores

            with sp.If(is_fast(sp) > 0):
                bases = [group_base(g) for g in range(2)]
                sp.wait_ge(q_stored, 16 * NCH)
                for g in range(2):
                    load_q(bases[g], g)
                with sp.Fori(0, (G - 3) // 2) as i:
                    load_group(i * 2 + 2, 0, i * 4 + 2)
                    load_group(i * 2 + 3, 1, i * 4 + 4)
                load_group(G - 1, (G - 1) % 2, 2 * (G - 1) - 2, REST)
                store_out(early_run, early_out)
            with sp.Else():
                sp.wait_ge(q_stored, 16 * NCH)
                sp.wait_ge(square_done, 2)
                for n in range(2):
                    sp.wait_ge(dist_loaded[n], 16)
                    sp.wait_ge(rel_loaded[n], 16)
                sp.wait_ge(src_stored, 16)
                with sp.Fori(0, FULL) as g:
                    general_loads(g, GROUP)
                general_loads(FULL, REST)

            sp.wait_ge(redo_set, 1)
            sp.wait_ge(early_out, 16 * EARLY)
            with sp.If(is_redo(sp) > 0):
                sp.wait_ge(late_out, 16 * store_out(redo_run, late_out))
            with sp.Else():
                sp.wait_ge(late_out, 16 * store_out(late_run, late_out))

        @block.gpsimd
        def _(pool):
            nc.gpsimd.memset(ident[:, :], 0.0).then_inc(pool_const, 1)
            pool.wait_ge(pool_const, 1)
            nc.gpsimd.affine_select(out=ident[:, :], in_=ident[:, :], compare_op=ALU.not_equal, fill=1.0,
                                    base=0, pattern=[[-1, P]], channel_multiplier=1).then_inc(pool_const, 1)
            nc.gpsimd.iota(lane_i[:, :], pattern=[[0, 1]], base=-WIN, channel_multiplier=1).then_inc(pool_const, 1)
            nc.gpsimd.iota(win_i[:, :], pattern=[[1, WIN]], base=0, channel_multiplier=0).then_inc(pool_const, 1)
            nc.gpsimd.iota(node_i[:, :], pattern=[[P, NB]], base=0, channel_multiplier=1).then_inc(pool_const, 1)
            nc.gpsimd.memset(ones_bf[:, :], 1.0).then_inc(pool_const, 1)
            nc.gpsimd.memset(ones_f[:, :], 1.0).then_inc(pool_const, 1)
            def gather(h, s, table=p_rows, tiles=HT):
                if early(h):
                    pool.wait_ge(first_index, 16)
                else:
                    pool.wait_ge(index_ready, h + 1)
                pool.sem_inc(index_seen, 1)
                for j in range(tiles):
                    nc.gpsimd.indirect_dma_start(
                        rows[:, s, j, :], None, table,
                        bass.IndirectOffsetOnAxis(ap=index[:, s, j:j + 1], axis=0)).then_inc(gathered[s], 16)

            for h in range(4):
                gather(h, h, x)
            pool.wait_ge(p_stored, 16 * NCH)
            for h in range(4, 8):
                gather(h, h)
            pool.wait_ge(base_done, 1)
            with pool.If(is_fast(pool) > 0):
                with pool.Fori(0, LOOPS - EARLY) as i:
                    for k in range(SLOTS):
                        gather(i * SLOTS + (8 + k), k, tiles=HT - 1 if k == HOT_HALF else HT)
                with pool.Fori(0, EARLY) as n:
                    for k in range(SLOTS):
                        gather(n * SLOTS + (FIRST_EARLY + k), k)
                gather(H - 2, (H - 2) % SLOTS)
                gather(H - 1, (H - 1) % SLOTS, tiles=LASTT)
                pool.wait_ge(early_up["rstd_done"], 1)
                for piece in early_run[0]:
                    divide(nc.gpsimd, piece).then_inc(early_up["res_done"], 1)
            with pool.Else():
                with pool.Fori(0, G) as g:
                    pool.wait_ge(gen_index_ready, g + 1)
                    pool.sem_inc(index_seen, 1)
                    for s in range(2):
                        for j in range(HT):
                            nc.gpsimd.indirect_dma_start(
                                rows[:, s, j, :], None, p_rows,
                                bass.IndirectOffsetOnAxis(ap=index[:, s, j:j + 1], axis=0)).then_inc(gen_gathered, 16)

        @block.tensor
        def _(pe):
            pe.wait_ge(pool_const, 2)
            def turn_table(table, ps, done, read=None):
                for j in range(GT):
                    mm = nc.tensor.transpose(bank[6 + j // 4][:, (j % 4) * G:(j % 4 + 1) * G],
                                             table[0:G, j * TILE:(j + 1) * TILE], ident[0:G, 0:G])
                mm.then_inc(ps, 1)

            def turn_x(c):
                bs = chunk_blocks[c]
                if c >= 2:
                    pe.wait_ge(xt_done, c - 1)
                for b in bs:
                    if b == 0:
                        pe.wait_ge(x_loaded[0], 16)
                    if b == XA:
                        pe.wait_ge(x_loaded[1], 16)
                    if b == XB:
                        pe.wait_ge(x_loaded[2], 32)
                    mm = nc.tensor.transpose(bank[c % 2][:, (b - bs.start) * P:(b - bs.start + 1) * P],
                                             xn[:, b, :], ident[:, :])
                mm.then_inc(xt_ps_done, 1)

            def times_x(c, w, banks, ps, done):
                if c >= 2:
                    pe.wait_ge(done, c - 1)
                for n, b in enumerate(chunk_blocks[c]):
                    mm = nc.tensor.matmul(banks[c % 2][:, n * D:(n + 1) * D], xt[:, b * P:(b + 1) * P], w[:, :],
                                          start=True, stop=True)
                mm.then_inc(ps, 1)

            turn_x(0)
            pe.wait_ge(w1a_loaded, 16)
            for c in range(NCH):
                if c + 1 < NCH:
                    turn_x(c + 1)
                pe.wait_ge(xt_done, c + 1)
                times_x(c, w1a, bank[2:4], p_ps, p_done)
                if c == 2:
                    pe.wait_ge(pool_const, 7)
                    pe.wait_ge(wide_done, 1)
                    nc.tensor.matmul(bank[4][:, 0:1], ones_f[0:G, :], wide[0:G, 0:1], start=True, stop=True).then_inc(wide_ps, 1)
            pe.wait_ge(src_done, 1)
            turn_table(src_f, src_ps, src_col_done)
            pe.wait_ge(w1b_loaded, 16)
            pe.wait_ge(base_done, 1)
            for c in range(NCH):
                times_x(c, w1b, bank[4:6], q_ps, q_done)
                if c == 3:
                    pe.wait_ge(src_col_done, 2)
                    pe.wait_ge(rel_done, 1)
                    turn_table(dst_f, tables_ps, tables_done)

            def turn_weights():
                pe.wait_ge(weights_loaded, 16 * 16)
                nc.tensor.transpose(bank[7][:, 0:D], w3[:, :], ident[:, :])
                nc.tensor.transpose(bank[7][:, D:2 * D], wu2[:, :], ident[:, :]).then_inc(turn_ps, 1)

            def fold_weights():
                pe.wait_ge(turned, 2)
                nc.tensor.matmul(bank[7][:, 0:D], w3t[:, :], wu1b[:, :], start=True, stop=True)
                nc.tensor.matmul(bank[7][:, D:2 * D], wu2t[:, :], wi1[:, :], start=True, stop=True)
                nc.tensor.matmul(bank[7][:, 2 * D:2 * D + 1], wu1b[:, :], cols[:, 0:1], start=True, stop=True)
                nc.tensor.matmul(bank[7][:, 2 * D + 1:2 * D + 2], wi1[:, :], cols[:, 1:2], start=True, stop=True).then_inc(fold_ps, 1)

            def update_x(c):
                n0, n = chunk[c]
                if c < 2:
                    pe.wait_ge(q_done, NCH if c % 2 == (NCH - 1) % 2 else NCH - 1)
                else:
                    pe.wait_ge(xu_done, c - 1)
                nc.tensor.matmul(bank[4 + c % 2][:, 0:n], wu1a[:, :], xt[:, n0:n0 + n], start=True, stop=True)\
                    .then_inc(xu_ps, 1)

            def turn_rows(h):
                pe.wait_ge(gathered[h], 16 * HT)
                if h >= 2:
                    pe.wait_ge(xg_ready, h - 1)
                for j in range(HT):
                    mm = nc.tensor.transpose(bank[h % 2][:, j * TILE:(j + 1) * TILE], rows[:, h, j, :], ident[:, :])
                mm.then_inc(xg_ps, 1)

            pe.wait_ge(tables_done, 2)
            turn_weights()
            for h in range(2):
                turn_rows(h)
            for c in range(NCH):
                update_x(c)
                if c == 2:
                    fold_weights()
            for h in range(2, 4):
                turn_rows(h)


            def first_layer(h, g2, g4, k, chunk_n):
                s, at, n = (k // 2) % 2, (k % 2) * HALF, half_edges(h)
                if later(h, 2):
                    pe.wait_ge(h1_ready, h - 1)
                elif h == 0:
                    pe.wait_ge(xg_ready, 4)
                ps = pre_ps[k % 2]
                if early(h):
                    nc.tensor.matmul(ps[:, :], w1a[:, :], xg[:, h, :], start=True, stop=True)
                else:
                    tiles = n // TILE
                    if hot_tile(h, k, chunk_n):
                        tiles = HT - 1
                        pe.wait_ge(src_hot_ready, g4 * HOT_PARTS)
                        for b in range(NB):
                            nc.tensor.matmul(ps[:, tiles * TILE:HALF], p_out[:, b, :], src_hot[:, b, :],
                                             start=b == 0, stop=True, skip_group_check=True)
                    before = g4 * (16 * HT)
                    if hot_tile(h, k, chunk_n):
                        before = g4 * (16 * (HT - 1)) + 16
                    elif k == HOT_HALF and later(h, SLOTS):
                        before = g4 * (16 * HT) - 16 * (LOOPS - EARLY)
                    pe.wait_ge(gathered[k], before + 16 * tiles)
                    for j in range(tiles):
                        nc.tensor.matmul(ps[:, j * TILE:(j + 1) * TILE], rows[:, k, j, :], ident[:, :], is_transpose=True,
                                         start=j == 0 and not hot_tile(h, k, chunk_n), stop=True, skip_group_check=True)
                pe.wait_ge(radial_ready, h + 1)
                if k % 2 == 0:
                    pe.wait_ge(q_loaded[s], g2 * 16 + 16)
                nc.tensor.matmul(ps[:, 0:n], left[:, s, :], feat[:, s, at:at + n], start=False, stop=True,
                                 skip_group_check=True).then_inc(pre_done, 1)

            def second_tiles(k, tiles):
                nc.tensor.matmul(l2_ps[k][:, 0:tiles * D], ones_bf[0:3, :],
                                 b2_rhs[:, 0:tiles, :].rearrange("p t d -> p (t d)"), start=True, stop=True)
                for j in range(tiles):
                    mm = nc.tensor.matmul(l2_ps[k][:, j * D:(j + 1) * D], h1[:, k, j * TILE:(j + 1) * TILE],
                                          w2half[:, :], start=False, stop=True, skip_group_check=True)
                return mm

            def second_layer(h, k):
                pe.wait_ge(h1_ready, h + 1)
                if not loops(h) and h == 0:
                    pe.wait_ge(b2_placed, 48)
                if later(h, 2):
                    pe.wait_ge(h2_ready, h - 1)
                second_tiles(k % 2, half_edges(h) // TILE).then_inc(l2_done, 1)

            def sum_tile(s, h2_tile, t):
                return nc.tensor.matmul(agg_ps[s][:, 0:WIN], h2_tile, hot[:, s, t, :],
                                        start=t == 0, stop=True, skip_group_check=True)

            def count_edges(s):
                return nc.tensor.matmul(agg_ps[s][:, WIN:2 * WIN], ones_bf[:, :],
                                        hot_count[:, s, :].bitcast(BF16)[:, 1:2 * WIN:2],
                                        start=False, stop=True, skip_group_check=True)

            def sum_over_dst(h, g, k):
                s, tiles = (k // 2) % 2, half_edges(h) // TILE
                pe.wait_ge(h2_ready, h + 1)
                if k % 2 == 0:
                    pe.wait_ge(hot_ready, g + 1)
                    if later(g, 2):
                        pe.wait_ge(z_added, g * 2 - 3)
                for j in range(tiles):
                    t = (k % 2) * HT + j
                    mm = sum_tile(s, h2[:, k % 2, j * D:(j + 1) * D], t)
                if k % 2 == 1:
                    pe.wait_ge(count_ready, g + 1)
                    mm = count_edges(s)
                mm.then_inc(seg_done, 1)

            def window_product(g, s):
                pe.wait_ge(win_ready, g + 1)
                if later(g, 1):
                    pe.wait_ge(z_added, g * 2 + 1)
                nc.tensor.matmul(bank[6][:, 0:WIN], w3u[:, :], win_sum[:, s, :], start=True, stop=True)\
                    .then_inc(win_ps, 1)

            def update_b(run, n):
                at, up = Place(run, n), run[1]
                pe.wait_ge(up["s1_done"], n + 1)
                if not loops(n) and n >= 2:
                    pe.wait_ge(up["t2_done"], n - 1)
                nc.tensor.matmul(at.b_bank[:, 0:at.size], wui[:, :], at.s1, start=True, stop=True).then_inc(up["b_ps"], 1)

            def update_c(run, n):
                at, up = Place(run, n), run[1]
                pe.wait_ge(up["s2_done"], n + 1)
                if not loops(n) and n >= 2:
                    pe.wait_ge(up["y_done"], n - 1)
                for j in range(at.count):
                    m = min(P, at.size - j * P)
                    mm = nc.tensor.matmul(at.c_bank[0:m, j * D:(j + 1) * D], at.s2[:, j * P:j * P + m],
                                          wi2c[:, :], start=True, stop=True)
                mm.then_inc(up["c_ps"], 1)

            def step(h, g, g2, g4, k, n=None):
                if loops(h) or h < H:
                    first_layer(h, g2, g4, k, n)
                if n is not None and k == 5:
                    update_c(early_run, n)
                if loops(h) or 1 <= h <= H:
                    second_layer(h - 1, (k - 1) % SLOTS)
                if k % 2 == 1 and later(h, 5):
                    window_product(g - 2, (k // 2) % 2)
                if loops(h) or 2 <= h <= H + 1:
                    sum_over_dst(h - 2, g - 1, (k - 2) % SLOTS)
                if n is not None and k == 2:
                    update_b(early_run, n)

            with pe.If(is_fast(pe) > 0):
                for h in range(8):
                    if h == 2:
                        pe.wait_ge(xu_done, NCH)
                    step(h, h // 2, h // 4, 0, h)
                with pe.Fori(0, LOOPS - EARLY) as i:
                    for k in range(SLOTS):
                        step(i * 8 + (8 + k), i * 4 + (4 + k // 2), i * 2 + (2 + k // 4), i + 1, k)
                with pe.Fori(0, EARLY) as n:
                    for k in range(SLOTS):
                        h = FIRST_EARLY + k
                        step(n * 8 + h, n * 4 + h // 2, n * 2 + h // 4, n + h // 8, k, n)
                for h in range(H - 2, H + 2):
                    step(h, h // 2, h // 4, h // 8, h % 8)
                window_product(G - 1, (G - 1) % 2)
            with pe.Else():
                pe.wait_ge(xu_done, NCH)
                pe.wait_ge(folded, 1)
                pe.wait_ge(b2_placed, 48)
                with pe.Fori(0, G) as g:
                    with pe.Fori(0, NW) as w:
                        pe.wait_ge(gen_gathered, g * (16 * GT) + 16 * GT)
                        pe.wait_ge(gen_radial_ready, g + 1)
                        pe.wait_ge(gen_q_loaded, (g * NW + w + 1) * 16)
                        pe.wait_ge(gen_hot_ready, g * NW + w + 1)
                        for s in range(2):
                            for j in range(HT):
                                nc.tensor.matmul(pre_ps[s][:, j * TILE:(j + 1) * TILE], rows[:, s, j, :], ident[:, :],
                                                 is_transpose=True, start=j == 0, stop=True, skip_group_check=True)
                            mm = nc.tensor.matmul(pre_ps[s][:, :], left[:, 0, :], feat[:, 0, s * HALF:(s + 1) * HALF],
                                                  start=False, stop=True, skip_group_check=True)
                        mm.then_inc(gen_pre_done, 1)
                        pe.wait_ge(gen_h1_ready, g * NW + w + 1)
                        for s in range(2):
                            mm = second_tiles(s, HT)
                        mm.then_inc(gen_l2_done, 1)
                        pe.wait_ge(gen_h2_ready, g * NW + w + 1)
                        for t in range(GT):
                            sum_tile(0, h2[:, t // HT, t % HT * D:(t % HT + 1) * D], t)
                        pe.wait_ge(gen_count_ready, g * NW + w + 1)
                        count_edges(0).then_inc(gen_seg_done, 1)
                        pe.wait_ge(gen_win_ready, g * NW + w + 1)
                        nc.tensor.matmul(bank[6][:, 0:WIN], w3u[:, :], win_sum[:, 0, :], start=True, stop=True)\
                            .then_inc(gen_win_ps, 1)

            def update(run):
                for n in range(len(run[0]) + 1):
                    if n < len(run[0]):
                        update_b(run, n)
                    if n >= 1:
                        update_c(run, n - 1)

            pe.wait_ge(redo_set, 1)
            pe.wait_ge(edges_done, 1)
            with pe.If(is_redo(pe) > 0):
                update(redo_run)
            with pe.Else():
                update(late_run)

        @block.scalar
        def _(act):
            act.wait_ge(pads_set, 1)
            act.dma_start(dst_i[0:FULL, :], dst_whole).then_inc(dst_loaded, 16)
            act.dma_start(dst_i[FULL:G, 0:REST], dst_rest).then_inc(dst_loaded, 16)
            act.wait_ge(pool_const, 3)
            nc.scalar.activation(lane[:, :], lane_i[:, :], ACT.Copy).then_inc(lane_done, 1)
            for c in range(NCH):
                n = len(chunk_blocks[c]) * P
                act.wait_ge(xt_ps_done, c + 1)
                nc.scalar.activation(xt[:, c * HALF:c * HALF + n], bank[c % 2][:, 0:n], ACT.Copy).then_inc(xt_done, 1)
                if c == 2:
                    act.wait_ge(edges_loaded, 32)
                    nc.scalar.activation(src_f[0:G, :], src_i[0:G, :], ACT.Copy).then_inc(src_done, 1)
            act.wait_ge(src_ps, 1)
            for q in range(2):
                nc.scalar.activation(src_col[:, 0:G, 4 * q:4 * q + 4],
                                     bank[6 + q][:, 0:4 * G].rearrange("p (j g) -> p g j", g=G), ACT.Copy)\
                    .then_inc(src_col_done, 1)
            for c in range(NCH):
                bs = chunk_blocks[c]
                act.wait_ge(q_ps, c + 1)
                nc.scalar.activation(q_out[:, bs.start:bs.stop, :],
                                     bank[4 + c % 2][:, 0:len(bs) * D].rearrange("p (b d) -> p b d", d=D), ACT.Copy)\
                    .then_inc(q_done, 1)

            def add_bu1(c):
                n0, n = chunk[c]
                act.wait_ge(xu_ps, c + 1)
                nc.scalar.activation(z[:, n0:n0 + n], bank[4 + c % 2][:, 0:n], ACT.Identity, bias=cols[:, 2:3])\
                    .then_inc(xu_done, 1)

            def squares(h, g2, k):
                s, at = (k // 2) % 2, (k % 2) * HALF
                act.wait_ge(dist_loaded[s], g2 * 16 + 16)
                act.wait_ge(rel_loaded[s], g2 * 16 + 16)
                nc.scalar.activation(feat[:, s, at:at + HALF], near[:, s, at:at + HALF],
                                     ACT.Square, bias=offset[:, :]).then_inc(square_done, 1)

            def gaussians(h, k):
                s, at = (k // 2) % 2, (k % 2) * HALF
                act.wait_ge(square_done, h + 1)
                nc.scalar.activation(feat[:, s, at:at + HALF], feat[:, s, at:at + HALF], ACT.Exp, scale=rate[:, :])\
                    .then_inc(radial_ready, 1)

            def first_tanh(run, n):
                at = Place(run, n)
                nc.scalar.activation(at.s1, z[:, at.cols], ACT.Tanh, scale=0.5).then_inc(run[1]["t1_done"], 1)

            def second_tanh(run, n):
                at, up = Place(run, n), run[1]
                act.wait_ge(up["b_ps"], n + 1)
                if not loops(n) and n >= 2:
                    act.wait_ge(up["s2_done"], n - 1)
                ps = at.b_bank[:, 0:at.size]
                nc.scalar.activation(tu[:, at.slot, 0:at.size], ps, ACT.Tanh, bias=bui_half[:, :], scale=0.5)
                nc.scalar.activation(at.s2, ps, ACT.Identity, bias=bui[:, :]).then_inc(up["t2_done"], 1)

            def squares_of_y(run, n):
                at, up = Place(run, n), run[1]
                act.wait_ge(up["y_done"], n + 1)
                if not loops(n) and n >= 2:
                    act.wait_ge(up["var_done"], n - 1)
                nc.scalar.activation(y2[0:at.nodes, at.slot, 0:at.count * D], y_flat[0:at.nodes, at.rows], ACT.Square)\
                    .then_inc(up["y2_done"], 1)

            def deviation(run):
                act.wait_ge(run[1]["var_done"], len(run[0]))
                bs = blocks_of(run)
                nc.scalar.activation(std[:, bs], var[:, bs], ACT.Sqrt, bias=eps[:, :], scale=1.0 / D)\
                    .then_inc(run[1]["std_done"], 1)

            def step(h, r, g2_next, k, n=None):
                if loops(h) or h < H:
                    size = half_edges(h)
                    act.wait_ge(pre_done, h + 1)
                    if later(h, 2):
                        act.wait_ge(h1_ready, h - 1)
                    nc.scalar.activation(th1[:, k % 2, 0:size], pre_ps[k % 2][:, 0:size], ACT.Tanh, scale=0.5)\
                        .then_inc(tanh1_done, 1)
                if loops(h) or h + 2 < H:
                    squares(h + 2, g2_next, (k + 2) % SLOTS)
                if loops(h) or 1 <= h <= H:
                    size = half_edges(h - 1)
                    act.wait_ge(l2_done, h)
                    if later(h, 3):
                        act.wait_ge(h2_ready, h - 2)
                    nc.scalar.activation(th2[:, (k - 1) % 2, 0:size], l2_ps[(k - 1) % 2][:, 0:size], ACT.Tanh, scale=0.5)\
                        .then_inc(tanh2_done, 1)
                if loops(h) or h + 2 < H:
                    gaussians(h + 2, (k + 2) % SLOTS)
                if k == HOT_HALF and n is None and (loops(h) or h < SLOTS):
                    if loops(h):
                        act.wait_ge(src_hot_ready, r * HOT_PARTS)
                    act.dma_start(src_b[:, :], src_rows[bass.ds(r * 4 + 4, 1), HALF * (HOT_HALF % 2) + HALF - TILE:
                                                        HALF * (HOT_HALF % 2) + HALF].broadcast_to([P, TILE]))\
                        .then_inc(src_b_loaded, 16)
                if n is not None and k == 0:
                    act.wait_ge(z_added, h - 3)
                    first_tanh(early_run, n)
                if n is not None and k == 3:
                    second_tanh(early_run, n)
                if n is not None and k == 6:
                    squares_of_y(early_run, n)

            act.wait_ge(lane_done, 2)
            for h in (0, 1):
                squares(h, 0, h)
                gaussians(h, h)
            def copy_turned(h):
                act.wait_ge(xg_ps, h + 1)
                nc.scalar.activation(xg[:, h, :], bank[h % 2][:, :], ACT.Copy).then_inc(xg_ready, 1)

            for h in range(2):
                copy_turned(h)
            act.wait_ge(weights_loaded, 16 * 16)
            for c in range(NCH):
                add_bu1(c)
            for h in range(2, 4):
                copy_turned(h)
            act.wait_ge(base_done, 1)
            with act.If(is_fast(act) > 0):
                for h in range(8):
                    if h == HOT_HALF:
                        act.wait_ge(src_stored, 16)
                    step(h, 0, (h + 2) // 4, h)
                with act.Fori(0, LOOPS - EARLY) as i:
                    for k in range(SLOTS):
                        step(i * 8 + (8 + k), i + 1, i * 2 + (2 + (k + 2) // 4), k)
                with act.Fori(0, EARLY) as n:
                    for k in range(SLOTS):
                        h = FIRST_EARLY + k
                        step(n * 8 + h, n + h // 8, n * 2 + (h + 2) // 4, k, n)
                for h in range(H - 2, H + 1):
                    step(h, h // 8, (h + 2) // 4, h % 8)
                deviation(early_run)
            with act.Else():
                with act.Fori(0, G) as g:
                    act.wait_ge(gen_dist_loaded, g * 16 + 16)
                    nc.scalar.activation(feat[0:RADIAL, 0, :], near[0:RADIAL, 0, :], ACT.Square,
                                         bias=offset[0:RADIAL, :]).then_inc(gen_square_done, 1)
                    act.wait_ge(gen_square_done, g + 1)
                    nc.scalar.activation(feat[0:RADIAL, 0, :], feat[0:RADIAL, 0, :], ACT.Exp,
                                         scale=rate[0:RADIAL, :]).then_inc(gen_radial_ready, 1)
                    with act.Fori(0, NW) as w:
                        act.wait_ge(gen_pre_done, g * NW + w + 1)
                        for s in range(2):
                            a = nc.scalar.activation(th1[:, s, :], pre_ps[s][:, :], ACT.Tanh, scale=0.5)
                        a.then_inc(gen_tanh1_done, 1)
                        act.wait_ge(gen_l2_done, g * NW + w + 1)
                        for s in range(2):
                            a = nc.scalar.activation(th2[:, s, :], l2_ps[s][:, :], ACT.Tanh, scale=0.5)
                        a.then_inc(gen_tanh2_done, 1)

            def update(run):
                act.wait_ge(edges_done, 1)
                for n in range(len(run[0]) + 2):
                    if n < len(run[0]):
                        first_tanh(run, n)
                    if 1 <= n <= len(run[0]):
                        second_tanh(run, n - 1)
                    if n >= 2:
                        squares_of_y(run, n - 2)
                deviation(run)

            act.wait_ge(redo_set, 1)
            with act.If(is_redo(act) > 0):
                act.wait_ge(early_out, 16 * EARLY)
                update(redo_run)
            with act.Else():
                update(late_run)

        @block.vector
        def _(dve):
            chain = [0]

            def link(ins):
                chain[0] += 1
                ins.then_inc(v_chain, 1)
                dve.wait_ge(v_chain, chain[0])

            nc.vector.memset(dst_i[:, REST:GROUP], FAR).then_inc(pads_set, 1)
            nc.vector.memset(src_i[:, REST:GROUP], 0).then_inc(pads_set, 1)
            nc.vector.memset(left[32:WIN, :, :], 0.0).then_inc(zeros_set, 1)
            nc.vector.memset(xn[:, NB - 1, :], 0.0).then_inc(pads_set, 1)
            nc.vector.memset(near[32:WIN, :, :], 0.0).then_inc(zeros_set, 1)
            nc.vector.memset(rate[:, :], -1000.0)
            nc.vector.memset(offset[:, :], 0.0)
            nc.vector.memset(src_col[:, G:G + 3, :], 0)
            nc.vector.memset(eps[:, :], EPS)
            nc.vector.memset(var[:, :], 1.0)

            dve.wait_ge(dst_loaded, 32)
            link(nc.vector.tensor_copy(dst_f[0:G, :], dst_i[0:G, :]))
            nc.vector.tensor_reduce(least[0:G, 0:1], dst_f[0:G, 0:REST], AX.X, ALU.min)
            nc.vector.tensor_reduce(least[0:FULL, 1:2], dst_f[0:FULL, REST:GROUP], AX.X, ALU.min)
            nc.vector.tensor_reduce(most[0:G, 0:1], dst_f[0:G, 0:REST], AX.X, ALU.max)
            link(nc.vector.tensor_reduce(most[0:FULL, 1:2], dst_f[0:FULL, REST:GROUP], AX.X, ALU.max))
            nc.vector.tensor_tensor(least[0:FULL, 0:1], least[0:FULL, 0:1], least[0:FULL, 1:2], ALU.min)
            link(nc.vector.tensor_tensor(most[0:FULL, 0:1], most[0:FULL, 0:1], most[0:FULL, 1:2], ALU.max))
            link(nc.vector.tensor_scalar(base[0:G, 0:1], least[0:G, 0:1], float(N - WIN), None, ALU.min))
            link(nc.vector.tensor_tensor(wide[0:G, 1:2], most[0:G, 0:1], base[0:G, 0:1], ALU.subtract))
            nc.vector.tensor_scalar(wide[0:G, 0:1], wide[0:G, 1:2], -1.0 if force_general else float(WIN), None, ALU.is_ge)\
                .then_inc(wide_done, 1)
            def copy_p(c):
                bs = chunk_blocks[c]
                dve.wait_ge(p_ps, c + 1)
                nc.vector.tensor_copy(p_out[:, bs.start:bs.stop, :],
                                      bank[2 + c % 2][:, 0:len(bs) * D].rearrange("p (b d) -> p b d", d=D)).then_inc(p_done, 1)

            for c in range(2):
                copy_p(c)
            dve.wait_ge(wide_ps, 1)
            link(nc.vector.tensor_scalar(base[:, 2:3], bank[4][:, 0:1], 0.0, None, ALU.is_equal))
            nc.vector.tensor_copy(sorted_i[:, :], base[:, 2:3])
            link(nc.vector.tensor_tensor(base[0:G, 1:2], base[0:G, 0:1], base[0:G, 2:3], ALU.mult))
            nc.vector.tensor_copy(base_i[0:G, :], base[0:G, 1:2]).then_inc(base_done, 1)
            copy_p(2)
            nc.vector.tensor_scalar(dst_f[0:G, :], dst_f[0:G, :], base[0:G, 1:2], None, ALU.subtract).then_inc(rel_done, 1)
            for c in range(3, NCH):
                copy_p(c)
            dve.wait_ge(src_col_done, 2)
            nc.vector.tensor_scalar(index[:, 4:8, :].rearrange("p s t -> p (s t)"),
                                    src_col[:, 2:4, :].rearrange("p g t -> p (g t)"), 0.0, None, ALU.add)\
                .then_inc(index_ready, 8)
            dve.wait_ge(pool_const, 7)
            dve.wait_ge(lane_done, 1)
            nc.vector.memset(rate[0:RADIAL, :], -0.5 / (CUTOFF / (RADIAL - 1)) ** 2)
            nc.vector.tensor_scalar(offset[WIN:P, :], lane[WIN:P, :], -1.0, None, ALU.mult)
            nc.vector.tensor_scalar(offset[0:RADIAL, :], lane[0:RADIAL, :], float(WIN), -CUTOFF / (RADIAL - 1), ALU.add, ALU.mult)\
                .then_inc(lane_done, 1)
            nc.vector.tensor_copy(win[:, :], win_i[:, :])
            nc.vector.tensor_copy(node[:, :], node_i[:, :])
            dve.wait_ge(b2_loaded, 16)
            link(nc.vector.tensor_copy(b2_part[:, 0, :], b2_row[:, :]))
            link(nc.vector.tensor_tensor(b2_left[:, 0, :], b2_row[:, :], b2_part[:, 0, :], ALU.subtract))
            link(nc.vector.tensor_copy(b2_part[:, 1, :], b2_left[:, 0, :]))
            link(nc.vector.tensor_tensor(b2_left[:, 1, :], b2_left[:, 0, :], b2_part[:, 1, :], ALU.subtract))
            nc.vector.tensor_copy(b2_part[:, 2, :], b2_left[:, 1, :]).then_inc(b2_loaded, 1)
            dve.wait_ge(tables_ps, 1)
            for q in range(2):
                nc.vector.tensor_copy(rel_col[:, 0:G, 4 * q:4 * q + 4],
                                      bank[6 + q][:, 0:4 * G].rearrange("p (j g) -> p g j", g=G)).then_inc(tables_done, 1)
            dve.wait_ge(weights_loaded, 16 * 16)
            nc.vector.tensor_scalar(w2half[:, :], w2[:, :], 0.5, None, ALU.mult)
            dve.wait_ge(tables_done, 2)

            def take_turned():
                dve.wait_ge(turn_ps, 1)
                nc.vector.tensor_scalar(w3t[:, :], bank[7][:, 0:D], 0.5, None, ALU.mult).then_inc(turned, 1)
                nc.vector.tensor_copy(wu2t[:, :], bank[7][:, D:2 * D]).then_inc(turned, 1)

            def take_folded():
                dve.wait_ge(fold_ps, 1)
                nc.vector.tensor_copy(w3u[:, :], bank[7][:, 0:D])
                nc.vector.tensor_scalar(wui[:, :], bank[7][:, D:2 * D], 0.5, None, ALU.mult)
                nc.vector.tensor_copy(b3u[:, :], bank[7][:, 2 * D:2 * D + 1])
                nc.vector.tensor_tensor(bui[:, :], bank[7][:, 2 * D + 1:2 * D + 2], cols[:, 3:4], ALU.add).then_inc(folded, 1)
                dve.wait_ge(folded, 1)
                nc.vector.tensor_scalar(bui_half[:, :], bui[:, :], 0.5, None, ALU.mult).then_inc(folded, 1)

            def center_wi2():
                link(nc.vector.tensor_reduce(wi2_mean[:, :], wi2[:, :], AX.X, ALU.add))
                link(nc.vector.tensor_scalar(wi2_mean[:, :], wi2_mean[:, :], 0.5 / D, None, ALU.mult))
                nc.vector.tensor_scalar(wi2c[:, :], wi2[:, :], 0.5, wi2_mean[:, 0:1], ALU.mult, ALU.subtract).then_inc(wi2_done, 1)

            def center_x(b0, b1):
                xb = xn[:, b0:b1, :]
                link(nc.vector.tensor_tensor(xb, xb, bi2_all[:, :].rearrange("p (a d) -> p a d", a=1)
                                             .broadcast_to([P, b1 - b0, D]), ALU.add))
                link(nc.vector.tensor_reduce(xb_mean[:, b0:b1], xb, AX.X, ALU.add))
                link(nc.vector.tensor_scalar(xb_mean[:, b0:b1], xb_mean[:, b0:b1], 1.0 / D, None, ALU.mult))
                nc.vector.tensor_tensor(xb, xb, xb_mean[:, b0:b1].rearrange("p (b a) -> p b a", a=1)
                                        .broadcast_to([P, b1 - b0, D]), ALU.subtract).then_inc(xb_done, 1)

            def take_index(h, g, k):
                nc.vector.tensor_scalar(index[:, k, :], src_col[:, bass.ds(g, 1), (k % 2) * HT:(k % 2 + 1) * HT]
                                        .rearrange("p a t -> p (a t)"), 0.0, None, ALU.add).then_inc(index_ready, 1)

            def hot_edges(g, s):
                nc.vector.tensor_tensor(hot[:, s, :, :],
                                        win[:, :].rearrange("p (a w) -> p a w", a=1).broadcast_to([P, GT, WIN]),
                                        rel_col[:, bass.ds(g, 1), :].rearrange("p a t -> p (a t)")
                                        .rearrange("p (t a) -> p t a", a=1).broadcast_to([P, GT, WIN]),
                                        ALU.is_equal).then_inc(hot_ready, 1)

            def count_hot(s):
                return nc.vector.tensor_reduce(hot_count[:, s, :], hot[:, s, :, :].rearrange("p t w -> p w t"), AX.X, ALU.add)

            def group_base(g):
                return dve.value_load(base_sb[0:1, bass.ds(g, 1)], min_val=0, max_val=N - WIN)

            def take_sums(g, s, b=None):
                b = group_base(g) if b is None else b
                if later(g, 1):
                    dve.wait_ge(z_added, g * 2 - 1)
                nc.vector.tensor_copy(win_sum[:, s, :], agg_ps[s][:, 0:WIN]).then_inc(win_ready, 1)
                at = z[:, bass.ds(b, WIN)]
                nc.vector.scalar_tensor_tensor(out=at, in0=agg_ps[s][:, WIN:2 * WIN], scalar=b3u[:, :], in1=at,
                                               op0=ALU.mult, op1=ALU.add).then_inc(z_added, 1)

            def add_window(g, s, b=None):
                b = group_base(g) if b is None else b
                dve.wait_ge(win_ps, g + 1)
                dve.wait_ge(z_added, g * 2 + (1 if not loops(g) and g == G - 1 else 2))
                at = z[:, bass.ds(b, WIN)]
                nc.vector.tensor_tensor(at, at, bank[6][:, 0:WIN], ALU.add).then_inc(z_added, 1)

            def first_silu(run, n):
                at = Place(run, n)
                dve.wait_ge(run[1]["t1_done"], n + 1)
                nc.vector.scalar_tensor_tensor(out=at.s1, in0=at.s1, scalar=1.0, in1=z[:, at.cols],
                                               op0=ALU.add, op1=ALU.mult).then_inc(run[1]["s1_done"], 1)

            def second_silu(run, n):
                at = Place(run, n)
                dve.wait_ge(run[1]["t2_done"], n + 1)
                nc.vector.scalar_tensor_tensor(out=at.s2, in0=tu[:, at.slot, 0:at.size], scalar=1.0, in1=at.s2,
                                               op0=ALU.add, op1=ALU.mult).then_inc(run[1]["s2_done"], 1)

            def add_x(run, n):
                at = Place(run, n)
                dve.wait_ge(run[1]["c_ps"], n + 1)
                nc.vector.tensor_tensor(y_flat[0:at.nodes, at.rows], x_flat[0:at.nodes, at.rows],
                                        at.c_bank[0:at.nodes, 0:at.count * D], ALU.add).then_inc(run[1]["y_done"], 1)

            def sum_squares(run, n):
                at = Place(run, n)
                dve.wait_ge(run[1]["y2_done"], n + 1)
                nc.vector.tensor_reduce(var[0:at.nodes, at.blocks], y2[0:at.nodes, at.slot, 0:at.count * D]
                                        .rearrange("p (b d) -> p b d", d=D), AX.X, ALU.add)\
                    .then_inc(run[1]["var_done"], 1)

            def invert(run):
                bs = blocks_of(run)
                dve.wait_ge(run[1]["std_done"], 1)
                nc.vector.reciprocal(rstd[:, bs], std[:, bs]).then_inc(run[1]["rstd_done"], 1)

            def hot_src(h, r, part):
                b0, b1 = NB * part // HOT_PARTS, NB * (part + 1) // HOT_PARTS
                dve.wait_ge(src_b_loaded, r * 16 + 16)
                nc.vector.tensor_tensor(src_hot[:, b0:b1, :],
                                        src_b[:, :].rearrange("p (a t) -> p a t", a=1).broadcast_to([P, b1 - b0, TILE]),
                                        node[:, b0:b1].rearrange("p (b a) -> p b a", a=1).broadcast_to([P, b1 - b0, TILE]),
                                        ALU.is_equal).then_inc(src_hot_ready, 1)

            def step(h, r, g, k, n=None):
                s = (k // 2) % 2
                if loops(h) or h < H:
                    size = half_edges(h)
                    dve.wait_ge(tanh1_done, h + 1)
                    if later(h, 2):
                        dve.wait_ge(l2_done, h - 1)
                    nc.vector.scalar_tensor_tensor(out=h1[:, k % 2, 0:size], in0=th1[:, k % 2, 0:size], scalar=1.0,
                                                   in1=pre_ps[k % 2][:, 0:size], op0=ALU.add, op1=ALU.mult).then_inc(h1_ready, 1)
                if loops(h) or h + 8 < H:
                    take_index(h + 8, g + 4, k)
                if k % 2 == 0:
                    if later(g, 2):
                        dve.wait_ge(seg_done, h - 2)
                        take_sums(g - 2, s)
                    if loops(g) or g < G:
                        hot_edges(g, s)
                if loops(h) or 1 <= h <= H:
                    size = half_edges(h - 1)
                    dve.wait_ge(tanh2_done, h)
                    if later(h, 3):
                        dve.wait_ge(seg_done, h - 2)
                    nc.vector.scalar_tensor_tensor(out=h2[:, (k - 1) % 2, 0:size], in0=th2[:, (k - 1) % 2, 0:size], scalar=1.0,
                                                   in1=l2_ps[(k - 1) % 2][:, 0:size], op0=ALU.add, op1=ALU.mult)\
                        .then_inc(h2_ready, 1)
                if k % 2 == 0 and later(g, 3):
                    add_window(g - 3, 1 - s)
                if k % 2 == 1 and (loops(g) or g < G):
                    dve.wait_ge(hot_ready, g + 1)
                    count_hot(s).then_inc(count_ready, 1)
                if k >= SLOTS - HOT_PARTS and n is None and (loops(h) or h < SLOTS):
                    hot_src(h, r, k - (SLOTS - HOT_PARTS))
                if n is not None and k == 1:
                    first_silu(early_run, n)
                if n is not None and k == 4:
                    second_silu(early_run, n)
                if n is not None and k == 5:
                    add_x(early_run, n)
                if n is not None and k == 7:
                    sum_squares(early_run, n)

            take_turned()
            center_wi2()
            for n in range(4):
                center_x(NB * n // 4, NB * (n + 1) // 4)
            take_folded()
            with dve.If(is_fast(dve) > 0):
                for h in range(8):
                    if h == 4:
                        dve.wait_ge(base_loaded, 16)
                        link(nc.vector.tensor_copy(base_f[:, :], base_sb[:, :]))
                        for n in range(EARLY):
                            low = nc.vector.tensor_reduce(lowest[:, 0, n:n + 1], base_f[:, pending[n]:G], AX.X, ALU.min)
                        link(low)
                        link(nc.vector.tensor_scalar(lowest[:, 1, :], lowest[:, 0, :],
                                                     0.0 if force_redo else 1.0 / HALF, None, ALU.mult))
                        link(nc.vector.tensor_tensor(lowest[:, 2, :], lowest[:, 1, :], win[0:1, 1:EARLY + 1], ALU.is_lt))
                        link(nc.vector.tensor_reduce(lowest[:, 0, 0:1], lowest[:, 2, :], AX.X, ALU.max))
                        nc.vector.tensor_copy(redo_i[:, :], lowest[:, 0, 0:1]).then_inc(redo_set, 1)
                        dve.wait_ge(xu_done, NCH)
                    step(h, 0, h // 2, h)
                with dve.Fori(0, LOOPS - EARLY) as i:
                    for k in range(SLOTS):
                        step(i * 8 + (8 + k), i + 1, i * 4 + (4 + k // 2), k)
                with dve.Fori(0, EARLY) as n:
                    for k in range(SLOTS):
                        h = FIRST_EARLY + k
                        step(n * 8 + h, n + h // 8, n * 4 + h // 2, k, n)
                for h in range(H - 2, H + 1):
                    step(h, h // 8, h // 2, h % 8)
                bases = [group_base(g) for g in (G - 2, G - 1)]
                dve.wait_ge(seg_done, H)
                take_sums(G - 1, (G - 1) % 2, bases[1])
                add_window(G - 2, G % 2, bases[0])
                add_window(G - 1, (G - 1) % 2, bases[1])
                dve.wait_ge(z_added, 2 * G)
                nc.vector.memset(wide[:, :], 0.0).then_inc(edges_done, 1)
                invert(early_run)
            with dve.Else():
                dve.wait_ge(xu_done, NCH)
                dve.wait_ge(gathered[0], 16 * HT)
                dve.wait_ge(gathered[1], 16 * HT)
                nc.vector.memset(wide[:, :], 0.0).then_inc(gen_added, 1)
                nc.vector.memset(redo_i[:, :], 1).then_inc(redo_set, 1)
                nc.vector.memset(lowest[:, :, :], 0.0).then_inc(early_out, 16 * EARLY)
                with dve.Fori(0, G) as g:
                    dve.wait_ge(gen_added, g * NW + 1)
                    nc.vector.tensor_scalar(index[:, 0:2, :].rearrange("p s t -> p (s t)"),
                                            src_col[:, bass.ds(g, 1), :].rearrange("p a t -> p (a t)"), 0.0, None,
                                            ALU.add).then_inc(gen_index_ready, 1)
                    nc.vector.tensor_scalar(rel_col[:, G, :], rel_col[:, bass.ds(g, 1), :].rearrange("p a t -> p (a t)"),
                                            0.0, None, ALU.add).then_inc(gen_rel_ready, 1)
                    with dve.Fori(0, NW) as w:
                        dve.wait_ge(gen_rel_loaded, g * 16 + 16)
                        dve.wait_ge(gen_rel_ready, g * (NW + 1) + w + 1)
                        nc.vector.tensor_scalar(feat[WIN:P, 0, :], near[WIN:P, 0, :], lane[WIN:P, :], None, ALU.is_equal)
                        nc.vector.tensor_tensor(hot[:, 0, :, :],
                                                win[:, :].rearrange("p (a w) -> p a w", a=1).broadcast_to([P, GT, WIN]),
                                                rel_col[:, G, :].rearrange("p (t a) -> p t a", a=1)
                                                .broadcast_to([P, GT, WIN]), ALU.is_equal).then_inc(gen_hot_ready, 1)
                        dve.wait_ge(gen_hot_ready, g * NW + w + 1)
                        count_hot(0).then_inc(gen_count_ready, 1)
                        nc.vector.tensor_scalar(near[WIN:P, 0, :], near[WIN:P, 0, :], float(WIN), None, ALU.subtract)
                        nc.vector.tensor_scalar(rel_col[:, G, :], rel_col[:, G, :], float(WIN), None, ALU.subtract)\
                            .then_inc(gen_rel_ready, 1)
                        dve.wait_ge(gen_tanh1_done, g * NW + w + 1)
                        for s in range(2):
                            m = nc.vector.scalar_tensor_tensor(out=h1[:, s, :], in0=th1[:, s, :], scalar=1.0,
                                                               in1=pre_ps[s][:, :], op0=ALU.add, op1=ALU.mult)
                        m.then_inc(gen_h1_ready, 1)
                        dve.wait_ge(gen_tanh2_done, g * NW + w + 1)
                        for s in range(2):
                            m = nc.vector.scalar_tensor_tensor(out=h2[:, s, :], in0=th2[:, s, :], scalar=1.0,
                                                               in1=l2_ps[s][:, :], op0=ALU.add, op1=ALU.mult)
                        m.then_inc(gen_h2_ready, 1)
                        dve.wait_ge(gen_seg_done, g * NW + w + 1)
                        nc.vector.tensor_copy(win_sum[:, 0, :], agg_ps[0][:, 0:WIN]).then_inc(gen_win_ready, 1)
                        at = z[:, bass.ds(w * WIN, WIN)]
                        nc.vector.scalar_tensor_tensor(out=at, in0=agg_ps[0][:, WIN:2 * WIN], scalar=b3u[:, :], in1=at,
                                                       op0=ALU.mult, op1=ALU.add).then_inc(z_added, 1)
                        dve.wait_ge(gen_win_ps, g * NW + w + 1)
                        dve.wait_ge(z_added, g * NW + w + 1)
                        nc.vector.tensor_tensor(at, at, bank[6][:, 0:WIN], ALU.add).then_inc(gen_added, 1)
                dve.wait_ge(gen_added, G * NW + 1)
                nc.vector.memset(wide[:, :], 0.0).then_inc(edges_done, 1)

            def update(run):
                n_chunks = len(run[0])
                for n in range(n_chunks + 3):
                    if n < n_chunks:
                        first_silu(run, n)
                    if 1 <= n <= n_chunks:
                        second_silu(run, n - 1)
                    if 2 <= n <= n_chunks + 1:
                        add_x(run, n - 2)
                    if n >= 3:
                        sum_squares(run, n - 3)
                invert(run)
                dve.wait_ge(run[1]["rstd_done"], 1)
                for piece in run[0]:
                    divide(nc.vector, piece).then_inc(run[1]["res_done"], 1)

            dve.wait_ge(redo_set, 1)
            with dve.If(is_redo(dve) > 0):
                update(redo_run)
            with dve.Else():
                update(late_run)


_INS = ['x', 'src', 'dst', 'edge_weight', 'L0_gnn_Wm1', 'L0_gnn_bm1', 'L0_gnn_Wm2', 'L0_gnn_bm2', 'L0_gnn_Wm3',
        'L0_gnn_bm3', 'L0_gnn_Wu1', 'L0_gnn_bu1', 'L0_gnn_Wu2', 'L0_gnn_bu2', 'L0_gnn_Wi1', 'L0_gnn_bi1',
        'L0_gnn_Wi2', 'L0_gnn_bi2']
_OUT = ((3125, 128), 'float32')


def kernel(**inputs):
    import numpy as _np
    import concourse.bacc as _bacc
    from concourse import mybir as _mybir
    from concourse.bass_utils import run_bass_kernel_spmd as _run

    nc = _bacc.Bacc("TRN2", target_bir_lowering=False, num_devices=1)
    arrays, args = {}, []
    for name in _INS:
        a = _np.ascontiguousarray(inputs[name])
        arrays[f"in_{name}_dram"] = a
        args.append(nc.dram_tensor(f"in_{name}_dram", a.shape, _mybir.dt.from_np(a.dtype), kind="ExternalInput").ap())
    out = nc.dram_tensor("out_0_dram", _OUT[0], _mybir.dt.from_np(_np.dtype(_OUT[1])), kind="ExternalOutput").ap()
    gnn_kernel(nc, *args, out)
    r = _run(nc, [arrays], core_ids=[0])
    return r.results[0]["out_0_dram"]
```
